# Optimizing a Trainium2 kernel written in Bass

```python
import numpy as np
import jax
import jax.numpy as jnp

def _softmax(x, axis=-1):
    return jax.nn.softmax(x, axis=axis)

def _gelu(x):
    return jax.nn.gelu(x, approximate=True)

def _silu(x):
    return jax.nn.silu(x)

def _sigmoid(x):
    return jax.nn.sigmoid(x)

def _layernorm(x, axis=-1, eps=1e-05):
    m = jnp.mean(x, axis=axis, keepdims=True)
    v = jnp.var(x, axis=axis, keepdims=True)
    return (x - m) / jnp.sqrt(v + eps)

def _scatter_add(tgt, idx, src, axis=0):
    return tgt.at[idx].add(src)

def _segment_sum(src, seg, n):
    return jax.ops.segment_sum(src, seg, n)
kernel_name = 'mk_adaln_d1_jaxref_r8_1d7159'

def setup_inputs(seed: int=0):
    np.random.seed(seed)
    _w = jnp.asarray

    def _L0_attn_setup():
        import jax, jax.numpy as jnp
        import numpy as np
        SEQ_LEN = 256
        DIM_EMB = 128
        DIM_K = 128
        DIM_V = 128
        BATCH = 4
        key = jax.random.key(seed)
        kx, kq, kk, kv, ko = jax.random.split(key, 5)
        s = DIM_EMB ** (-0.5)
        return {'x': jax.random.normal(kx, (BATCH, SEQ_LEN, DIM_EMB), dtype=jnp.float32), 'Wq': jax.random.normal(kq, (DIM_EMB, DIM_K), dtype=jnp.float32) * s, 'Wk': jax.random.normal(kk, (DIM_EMB, DIM_K), dtype=jnp.float32) * s, 'Wv': jax.random.normal(kv, (DIM_EMB, DIM_V), dtype=jnp.float32) * s, 'Wo': jax.random.normal(ko, (DIM_V, DIM_V), dtype=jnp.float32) * DIM_V ** (-0.5)}
    _L0_attn_in = _L0_attn_setup()

    def _L0_ffn_setup():
        import jax, jax.numpy as jnp
        import numpy as np
        DIM = 128
        DEPTH = 6
        HEADS = 16
        DIM_HEAD = 64
        WINDOW = 32
        INNER = HEADS * DIM_HEAD
        DIM_INNER = int(DIM * 4 * 2 / 3)
        QK_SCALE = 8.0

        def shift_tokens(t):
            a, s = jnp.split(t, 2, -1)
            s = jnp.pad(s, ((0, 0), (1, 0), (0, 0)))[:, :-1]
            return jnp.concatenate([a, s], -1)

        def l2norm(t):
            return t / jnp.maximum(jnp.linalg.norm(t, axis=-1, keepdims=True), 1e-12)

        def rotate_half(x):
            x1, x2 = jnp.split(x, 2, -1)
            return jnp.concatenate([-x2, x1], -1)

        def rotary_tables(n):
            half = jnp.arange(0, DIM_HEAD, 2, dtype=jnp.float32)
            inv_freq = 1.0 / 10000.0 ** (half / DIM_HEAD)
            t = jnp.arange(n, dtype=jnp.float32)
            freqs = t[:, None] * inv_freq[None, :]
            freqs = jnp.concatenate([freqs, freqs], -1)
            base_scale = (half + 0.4 * DIM_HEAD) / (1.4 * DIM_HEAD)
            power = (t - n // 2) / (WINDOW // 2)
            scale = base_scale[None, :] ** power[:, None]
            scale = jnp.concatenate([scale, scale], -1)
            return (freqs, scale)

        def local_attention(q, k, v):
            b, h, n, d = q.shape
            w = WINDOW
            nw = n // w
            bq = q.reshape(b, h, nw, w, d)
            bk = k.reshape(b, h, nw, w, d)
            bv = v.reshape(b, h, nw, w, d)

            def look(t):
                p = jnp.pad(t, ((0, 0), (0, 0), (1, 0), (0, 0), (0, 0)))
                return jnp.concatenate([p[:, :, :nw], p[:, :, 1:]], axis=3)
            bk2, bv2 = (look(bk), look(bv))
            seq = jnp.arange(n).reshape(nw, w)
            seq_p = jnp.pad(seq, ((1, 0), (0, 0)), constant_values=-1)
            jt = jnp.concatenate([seq_p[:nw], seq_p[1:]], axis=1)
            it = seq[:, :, None]
            jb = jt[:, None, :]
            mask = (it < jb) | (it > jb + w) | (jb == -1)
            sim = jnp.einsum('bhwie,bhwje->bhwij', bq, bk2) * QK_SCALE
            sim = jnp.where(mask, -jnp.finfo(sim.dtype).max, sim)
            attn = jax.nn.softmax(sim, -1)
            out = jnp.einsum('bhwij,bhwje->bhwie', attn, bv2)
            return out.reshape(b, h, n, d)

        def attn_layer(x, Wqkv, qs, ksc, Wo):
            b, n, _ = x.shape
            qkv = x @ Wqkv
            q, k, v = jnp.split(qkv, 3, -1)
            sh = lambda t: t.reshape(b, n, HEADS, DIM_HEAD).transpose(0, 2, 1, 3)
            q, k, v = (sh(q), sh(k), sh(v))
            q = l2norm(q) * qs
            k = l2norm(k) * ksc
            freqs, scale = rotary_tables(n)
            cos, sin = (jnp.cos(freqs), jnp.sin(freqs))
            q = q * cos * scale + rotate_half(q) * sin * scale
            inv = 1.0 / scale
            k = k * cos * inv + rotate_half(k) * sin * inv
            out = local_attention(q, k, v)
            out = out.transpose(0, 2, 1, 3).reshape(b, n, INNER)
            return out @ Wo

        def ffn_layer(x, g, bln, W1, b1, W2, b2):
            mu = x.mean(-1, keepdims=True)
            var = ((x - mu) ** 2).mean(-1, keepdims=True)
            xn = (x - mu) / jnp.sqrt(var + 1e-05) * g + bln
            hg = xn @ W1 + b1
            a, gate = jnp.split(hg, 2, -1)
            return a * jax.nn.gelu(gate, approximate=False) @ W2 + b2
        key = jax.random.key(seed)
        ks = jax.random.split(key, 8)
        B, N = (2, 256)
        init = lambda k, shape: jax.random.normal(k, shape, jnp.float32) * 0.02
        return {'x': jax.random.normal(ks[0], (B, N, DIM), jnp.float32), 'Wqkv': init(ks[1], (DEPTH, DIM, 3 * INNER)), 'q_scale': jnp.ones((DEPTH, DIM_HEAD), jnp.float32), 'k_scale': jnp.ones((DEPTH, DIM_HEAD), jnp.float32), 'Wo': init(ks[2], (DEPTH, INNER, DIM)), 'ln_g': jnp.ones((DEPTH, DIM), jnp.float32), 'ln_b': jnp.zeros((DEPTH, DIM), jnp.float32), 'W1': init(ks[3], (DEPTH, DIM, 2 * DIM_INNER)), 'b1': jnp.zeros((DEPTH, 2 * DIM_INNER), jnp.float32), 'W2': init(ks[4], (DEPTH, DIM_INNER, DIM)), 'b2': jnp.zeros((DEPTH, DIM), jnp.float32)}
    _L0_ffn_in = _L0_ffn_setup()
    _L0_c = _w((lambda *s: np.random.randn(*s).astype(np.float32) * 0.05)(16, 128))
    _L0_wmod = _w((lambda *s: np.random.randn(*s).astype(np.float32) * 0.05)(128, 6 * 128) * 128 ** (-0.5))
    _d = {'L0_attn_x': _L0_attn_in['x'], 'L0_attn_Wq': _L0_attn_in['Wq'], 'L0_attn_Wk': _L0_attn_in['Wk'], 'L0_attn_Wv': _L0_attn_in['Wv'], 'L0_attn_Wo': _L0_attn_in['Wo'], 'L0_ffn_Wqkv': _L0_ffn_in['Wqkv'], 'L0_ffn_q_scale': _L0_ffn_in['q_scale'], 'L0_ffn_k_scale': _L0_ffn_in['k_scale'], 'L0_ffn_Wo': _L0_ffn_in['Wo'], 'L0_ffn_ln_g': _L0_ffn_in['ln_g'], 'L0_ffn_ln_b': _L0_ffn_in['ln_b'], 'L0_ffn_W1': _L0_ffn_in['W1'], 'L0_ffn_b1': _L0_ffn_in['b1'], 'L0_ffn_W2': _L0_ffn_in['W2'], 'L0_ffn_b2': _L0_ffn_in['b2'], 'L0_c': _L0_c, 'L0_wmod': _L0_wmod}
    _x0 = _d['L0_attn_x']
    _d['L0_attn_x'] = jax.random.normal(jax.random.fold_in(jax.random.key(seed), 1), (16, 256, 128), dtype=_x0.dtype)
    del _x0
    return _d

def reference(L0_attn_x, L0_attn_Wq, L0_attn_Wk, L0_attn_Wv, L0_attn_Wo, L0_ffn_Wqkv, L0_ffn_q_scale, L0_ffn_k_scale, L0_ffn_Wo, L0_ffn_ln_g, L0_ffn_ln_b, L0_ffn_W1, L0_ffn_b1, L0_ffn_W2, L0_ffn_b2, L0_c, L0_wmod):

    def _L0_attn_ref(x, Wq, Wk, Wv, Wo):
        import jax, jax.numpy as jnp
        import numpy as np
        SEQ_LEN = 256
        DIM_EMB = 128
        DIM_K = 128
        DIM_V = 128
        BATCH = 4
        q = jnp.einsum('bse,ek->bsk', x, Wq)
        k = jnp.einsum('bse,ek->bsk', x, Wk)
        v = jnp.einsum('bse,ev->bsv', x, Wv)
        scores = jnp.einsum('bqk,bsk->bqs', q, k)
        S = scores.shape[-1]
        causal_mask = jnp.triu(jnp.ones((S, S), dtype=bool), k=1)
        scores = jnp.where(causal_mask[None], -jnp.inf, scores)
        attn = jax.nn.softmax(scores * Wq.shape[1] ** (-0.5), axis=-1)
        out = jnp.einsum('bqs,bsv->bqv', attn, v)
        return jnp.einsum('bqv,vo->bqo', out, Wo)

    def _L0_ffn_ref(x, Wqkv, q_scale, k_scale, Wo, ln_g, ln_b, W1, b1, W2, b2):
        import jax, jax.numpy as jnp
        import numpy as np
        DIM = 128
        DEPTH = 6
        HEADS = 16
        DIM_HEAD = 64
        WINDOW = 32
        INNER = HEADS * DIM_HEAD
        DIM_INNER = int(DIM * 4 * 2 / 3)
        QK_SCALE = 8.0

        def shift_tokens(t):
            a, s = jnp.split(t, 2, -1)
            s = jnp.pad(s, ((0, 0), (1, 0), (0, 0)))[:, :-1]
            return jnp.concatenate([a, s], -1)

        def l2norm(t):
            return t / jnp.maximum(jnp.linalg.norm(t, axis=-1, keepdims=True), 1e-12)

        def rotate_half(x):
            x1, x2 = jnp.split(x, 2, -1)
            return jnp.concatenate([-x2, x1], -1)

        def rotary_tables(n):
            half = jnp.arange(0, DIM_HEAD, 2, dtype=jnp.float32)
            inv_freq = 1.0 / 10000.0 ** (half / DIM_HEAD)
            t = jnp.arange(n, dtype=jnp.float32)
            freqs = t[:, None] * inv_freq[None, :]
            freqs = jnp.concatenate([freqs, freqs], -1)
            base_scale = (half + 0.4 * DIM_HEAD) / (1.4 * DIM_HEAD)
            power = (t - n // 2) / (WINDOW // 2)
            scale = base_scale[None, :] ** power[:, None]
            scale = jnp.concatenate([scale, scale], -1)
            return (freqs, scale)

        def local_attention(q, k, v):
            b, h, n, d = q.shape
            w = WINDOW
            nw = n // w
            bq = q.reshape(b, h, nw, w, d)
            bk = k.reshape(b, h, nw, w, d)
            bv = v.reshape(b, h, nw, w, d)

            def look(t):
                p = jnp.pad(t, ((0, 0), (0, 0), (1, 0), (0, 0), (0, 0)))
                return jnp.concatenate([p[:, :, :nw], p[:, :, 1:]], axis=3)
            bk2, bv2 = (look(bk), look(bv))
            seq = jnp.arange(n).reshape(nw, w)
            seq_p = jnp.pad(seq, ((1, 0), (0, 0)), constant_values=-1)
            jt = jnp.concatenate([seq_p[:nw], seq_p[1:]], axis=1)
            it = seq[:, :, None]
            jb = jt[:, None, :]
            mask = (it < jb) | (it > jb + w) | (jb == -1)
            sim = jnp.einsum('bhwie,bhwje->bhwij', bq, bk2) * QK_SCALE
            sim = jnp.where(mask, -jnp.finfo(sim.dtype).max, sim)
            attn = jax.nn.softmax(sim, -1)
            out = jnp.einsum('bhwij,bhwje->bhwie', attn, bv2)
            return out.reshape(b, h, n, d)

        def attn_layer(x, Wqkv, qs, ksc, Wo):
            b, n, _ = x.shape
            qkv = x @ Wqkv
            q, k, v = jnp.split(qkv, 3, -1)
            sh = lambda t: t.reshape(b, n, HEADS, DIM_HEAD).transpose(0, 2, 1, 3)
            q, k, v = (sh(q), sh(k), sh(v))
            q = l2norm(q) * qs
            k = l2norm(k) * ksc
            freqs, scale = rotary_tables(n)
            cos, sin = (jnp.cos(freqs), jnp.sin(freqs))
            q = q * cos * scale + rotate_half(q) * sin * scale
            inv = 1.0 / scale
            k = k * cos * inv + rotate_half(k) * sin * inv
            out = local_attention(q, k, v)
            out = out.transpose(0, 2, 1, 3).reshape(b, n, INNER)
            return out @ Wo

        def ffn_layer(x, g, bln, W1, b1, W2, b2):
            mu = x.mean(-1, keepdims=True)
            var = ((x - mu) ** 2).mean(-1, keepdims=True)
            xn = (x - mu) / jnp.sqrt(var + 1e-05) * g + bln
            hg = xn @ W1 + b1
            a, gate = jnp.split(hg, 2, -1)
            return a * jax.nn.gelu(gate, approximate=False) @ W2 + b2
        for i in range(DEPTH):
            x = attn_layer(shift_tokens(x), Wqkv[i], q_scale[i], k_scale[i], Wo[i]) + x
            x = ffn_layer(shift_tokens(x), ln_g[i], ln_b[i], W1[i], b1[i], W2[i], b2[i]) + x
        return x
    x = L0_attn_x
    mod = (_silu(L0_c) @ L0_wmod).reshape(L0_c.shape[0], 6, 1, -1)
    sa, ca, ga, sb, cb, gb = (mod[:, 0], mod[:, 1], mod[:, 2], mod[:, 3], mod[:, 4], mod[:, 5])
    ga = (2 * (ga >= 0) - 1) * jnp.maximum(jnp.abs(ga), 0.25)
    gb = (2 * (gb >= 0) - 1) * jnp.maximum(jnp.abs(gb), 0.25)
    h = _layernorm(x, axis=-1) * (1 + ca) + sa
    x = x + ga * _L0_attn_ref(h, L0_attn_Wq, L0_attn_Wk, L0_attn_Wv, L0_attn_Wo)
    h = _layernorm(x, axis=-1) * (1 + cb) + sb
    x = x + gb * _L0_ffn_ref(h, L0_ffn_Wqkv, L0_ffn_q_scale, L0_ffn_k_scale, L0_ffn_Wo, L0_ffn_ln_g, L0_ffn_ln_b, L0_ffn_W1, L0_ffn_b1, L0_ffn_W2, L0_ffn_b2)
    return x

_drawn_inputs = setup_inputs


def setup_inputs(seed=0):
    import zlib

    import numpy as np

    out = dict(_drawn_inputs(seed))
    spreads = {'L0_ffn_q_scale': (1.0, 0.6),
     'L0_ffn_k_scale': (1.0, 0.6),
     'L0_ffn_ln_g': (1.0, 0.6),
     'L0_ffn_ln_b': (0.0, 0.8),
     'L0_ffn_b1': (0.0, 0.8),
     'L0_ffn_b2': (0.0, 0.663)}
    factors = {'L0_ffn_W1': 7.455, 'L0_ffn_W2': 7.323}
    for name, (base, spread) in spreads.items():
        noise = np.random.default_rng([zlib.crc32(name.encode()), seed]).standard_normal(out[name].shape)
        drawn = base * np.exp(spread * noise) if base else spread * noise
        out[name] = jnp.asarray(drawn.astype(out[name].dtype))
    for name, factor in factors.items():
        out[name] = (out[name] * factor).astype(out[name].dtype)
    return out
```

```python
from contextlib import ExitStack

import numpy as np
import concourse.bass as bass
from concourse import mybir

F32 = mybir.dt.float32
BF16 = mybir.dt.bfloat16
ACT = mybir.ActivationFunctionType
ALU = mybir.AluOpType
AX = mybir.AxisListType

P = 128
D = 128
B, S = 16, 256
TPB = S // P
NT = B * TPB
DEPTH = 6
H, DH = 16, 64
INNER = H * DH
PAIRS = H // 2
WIN = 32
WIDE = WIN + P
F = 341
FCH = [(0, 128), (128, 128), (256, 85)]
HPC = 8
CH = HPC * DH
KQ = 4
AT = NT + 1
FT = 4
MASKED = -3.0e38
EPS = 1e-5
RMS_SCALE = float(D) ** -0.5
POOL_SETUP = 7
QK_SCALE = 8.0
ATT1_SCALE = float(D) ** -0.5
CR = 2
CHUNK_COL = [INNER, INNER + CH, 0, CH, 2 * INNER, 2 * INNER + CH]


def build(nc, a_x, a_wq, a_wk, a_wv, a_wo, f_wqkv, f_qs, f_ks, f_wo, f_g, f_b, f_w1, f_b1, f_w2, f_b2,
          c_in, wmod, ident_in, masks_in, center_in, rope_in, out):
    with ExitStack() as ctx:
        def sb(name, shape, dt=F32):
            return ctx.enter_context(nc.sbuf_tensor(name, shape, dt))

        def sem(name):
            return ctx.enter_context(nc.semaphore(name))

        bank = [ctx.enter_context(nc.psum_tensor(f"bank{i}", [P, 512], F32)) for i in range(8)]

        ident = sb("ident", [P, P])
        identb = sb("identb", [P, P], BF16)
        mask_f = sb("mask_f", [P, P + WIDE + P])
        masks = sb("masks", [P, P + WIDE + P], BF16)
        mask_even, mask_odd, mask_causal = masks[:, 0:P], masks[:, P:P + WIDE], masks[:, P + WIDE:]
        center = sb("center", [P, P])
        rope = sb("rope", [P, 4, TPB, DH])
        neg_half = sb("neg_half", [P, HPC])
        eps = sb("eps", [P, HPC])
        x = sb("x", [P, AT, D])
        x1 = sb("x1", [P, NT, D])
        gb = sb("gb", [P, B, D])
        w1q, w1k, w1v, w1o = (sb(f"w1{n}", [P, D]) for n in "qkvo")
        wmod_s = sb("wmod_s", [P, 6 * D])
        crow = sb("crow", [B, D])
        cT = sb("cT", [P, B])
        csig = sb("csig", [P, B])
        cden = sb("cden", [P, B])
        cinv = sb("cinv", [P, B])
        csilu = sb("csilu", [P, B])
        cb_l = sb("cb_l", [P, P])
        mod = sb("mod", [P, 6, D])
        gate_sign = sb("gate_sign", [P, 2, D])
        gate_pos = sb("gate_pos", [P, 2, D])
        gate_abs = sb("gate_abs", [P, 2, D])
        tsum = sb("tsum", [P, TPB])
        nmean = sb("nmean", [P, TPB])
        xc = sb("xc", [P, TPB, D])
        sqj = sb("sqj", [P, TPB, D])
        ssq = sb("ssq", [P, TPB])
        var1 = sb("var1", [P, TPB])
        rstd = sb("rstd", [P, TPB])
        h1 = sb("h1", [P, TPB, D])
        h1s = sb("h1s", [P, TPB, D])
        ga = sb("ga", [P, D])
        xn = sb("xn", [P, TPB, D])
        h1T = sb("h1T", [P, S])
        q1T = sb("q1T", [P, S])
        k1T = sb("k1T", [P, S])
        v1 = sb("v1", [P, TPB, D])
        nm1 = sb("nm1", [P, TPB])
        nms1 = sb("nms1", [P, TPB])
        sum1 = sb("sum1", [P, TPB])
        rin1 = sb("rin1", [P, TPB])
        p1 = sb("p1", [P, P + S])
        p1T = sb("p1T", [P, 3 * P])
        o1T = sb("o1T", [P, S])
        att1 = sb("att1", [P, TPB, D])
        wqkv = sb("wqkv", [P, 3 * INNER])
        wo = sb("wo", [P, PAIRS, D])
        scales = sb("scales", [P, 2, DH])
        tables = sb("tables", [P, 4, TPB, DH])
        w1 = sb("w1", [P, 2 * F])
        w1g = sb("w1g", [P, 2 * F])
        w1c = sb("w1c", [P, 2 * F])
        w2 = sb("w2", [P, 3, D])
        lng = sb("lng", [P, 1])
        lnb = sb("lnb", [P, 1])
        lnb_l = sb("lnb_l", [P, P])
        b1r = sb("b1r", [P, 2 * F])
        b2r = sb("b2r", [P, D])
        bias1 = sb("bias1", [P, 2 * F])
        xs = sb("xs", [P, D])
        yT = sb("yT", [P, S + 1])
        sq = sb("sq", [P, 2, CH])
        rc = sb("rc", [P, 2, CH])
        rs = sb("rs", [P, 2, CH])
        rsum = sb("rsum", [P, 2, CH])
        rot = sb("rot", [P, 2, CH])
        n2 = sb("n2", [P, KQ, HPC])
        n2g = sb("n2g", [P, KQ, HPC])
        rn = sb("rn", [P, KQ, HPC])
        qT = sb("qT", [P, 2, 2, PAIRS, P])
        kTe = sb("kTe", [P, PAIRS, P])
        kTo = sb("kTo", [P, PAIRS, WIDE])
        v = sb("v", [P, 2, INNER])
        vt = sb("vt", [WIN, INNER])
        nmax = sb("nmax", [P, 2, 2])
        psm = sb("psm", [P, 2, 2])
        pinv = sb("pinv", [P, 2, 2])
        pr = sb("pr", [P, 2, 2, WIDE])
        pT = sb("pT", [P, 2, 2 * P + 2 * WIN])
        oT = sb("oT", [P, PAIRS, P])
        xsf = sb("xsf", [P, FT, D])
        xbf = sb("xbf", [P, FT, D])
        yTf = sb("yTf", [P, FT // 2, S + 1])
        sqf = sb("sqf", [P, FT, D])
        ssf = sb("ssf", [P, FT])
        vaf = sb("vaf", [P, FT])
        rsf = sb("rsf", [P, FT])
        ha = sb("ha", [P, 2, F])
        hg = sb("hg", [P, 2, F])
        gg = sb("gg", [P, 2, F])
        hm = sb("hm", [P, 2, F])
        hT = sb("hT", [P, 2, 3 * P])

        const_in, out_done, attn_w_in, ffn_w_in = (sem(n) for n in ("const_in", "out_done", "attn_w_in", "ffn_w_in"))
        pool_setup, dve_setup, pe_setup, act_setup = (sem(n) for n in ("pool_setup", "dve_setup", "pe_setup", "act_setup"))
        m_act, m_dve, m_pe, m_pool = (sem(n) for n in ("m_act", "m_dve", "m_pe", "m_pool"))
        x_full = sem("x_full")
        tables_done = sem("tables_done")
        xs_ready, xT_done, yT_ready = (sem(n) for n in ("xs_ready", "xT_done", "yT_ready"))
        chunk_done, sq_done, prod_done, red_done = (sem(n) for n in ("chunk_done", "sq_done", "prod_done", "red_done"))
        rsum_done, guard_done, rn_done, rot_done = (sem(n) for n in ("rsum_done", "guard_done", "rn_done", "rot_done"))
        rot_turned, t_copied, v_done = (sem(n) for n in ("rot_turned", "t_copied", "v_done"))
        ktail_done, vtail_done = sem("ktail_done"), sem("vtail_done")
        sims_done, max_done, exp_done, inv_done, norm_done = (
            sem(n) for n in ("sims_done", "max_done", "exp_done", "inv_done", "norm_done"))
        pt_done, pt_copied, pv_done, o_copied, wo_done, x_upd = (
            sem(n) for n in ("pt_done", "pt_copied", "pv_done", "o_copied", "wo_done", "x_upd"))
        w1g_done, w1c_mm, w1c_done, bias_mm, bias_done = (
            sem(n) for n in ("w1g_done", "w1c_mm", "w1c_done", "bias_mm", "bias_done"))
        f_xs, f_xT, f_yT, f_yc, f_ss, f_var, f_rstd = (
            sem(n) for n in ("f_xs", "f_xT", "f_yT", "f_yc", "f_ss", "f_var", "f_rstd"))
        f_h, f_hb, f_gelu, f_hm, f_hT, f_hTc, f_z = (
            sem(n) for n in ("f_h", "f_hb", "f_gelu", "f_hm", "f_hT", "f_hTc", "f_z"))
        scaled, gated = sem("scaled"), sem("gated")

        G = [bank[0], bank[1]]
        T = bank[2]
        SIM = [bank[3], bank[4]]
        PT = bank[5]
        O = bank[6]
        Z = bank[7]
        FH = [(bank[5], bank[6]), (bank[0], bank[1])]
        FT_B, FYC, FHT, FZ = bank[2], bank[3], bank[4], bank[7]

        N_CONST, N_ATTN, N_FFN = 12, 4, 7
        NF = NT // FT
        DA, AA, PA, GA = 26, 12, 7, 4

        def settle(eng):
            eng.wait_ge(pool_setup, POOL_SETUP)

        block = ctx.enter_context(nc.Block())

        @block.sync
        def _(sp):
            x_dram = a_x.rearrange("b (t p) d -> p (b t) d", p=P)
            o_dram = out.rearrange("b (t p) d -> p (b t) d", p=P)
            for dst, src in ((crow[:], c_in), (ident[:], ident_in), (wmod_s[:], wmod), (mask_f[:], masks_in),
                             (w1q[:], a_wq), (w1k[:], a_wk), (w1v[:], a_wv), (w1o[:], a_wo),
                             (center[:], center_in), (rope[:], rope_in)):
                sp.dma_start(dst, src).then_inc(const_in, 16)
            for i in range(2):
                half = slice(i * NT // 2, (i + 1) * NT // 2)
                sp.dma_start(x1[:, half, :], x_dram[:, half, :]).then_inc(const_in, 16)
            with sp.Fori(0, DEPTH) as L:
                sp.wait_ge(v_done, L * (2 * AT) + CR)
                sp.wait_ge(prod_done, L * (KQ * AT) + CR)
                sp.wait_ge(x_upd, L * NT + CR)
                sp.dma_start(wqkv[:], f_wqkv[bass.ds(L, 1)].rearrange("l p n -> p (l n)")).then_inc(attn_w_in, 16)
                sp.dma_start(wo[:], f_wo[bass.ds(L, 1)].rearrange("l (c p) n -> p (l c) n", p=P)).then_inc(attn_w_in, 16)
                sp.dma_start(scales[:, 0, :], f_ks[bass.ds(L, 1)].to_broadcast([P, DH])).then_inc(attn_w_in, 16)
                sp.dma_start(scales[:, 1, :], f_qs[bass.ds(L, 1)].to_broadcast([P, DH])).then_inc(attn_w_in, 16)
                sp.wait_ge(x_full, (L + 1) * B)
                sp.dma_start(w1[:], f_w1[bass.ds(L, 1)].rearrange("l p n -> p (l n)")).then_inc(ffn_w_in, 16)
                sp.dma_start(w2[:, 0:2, :], f_w2[bass.ds(L, 1), 0:2 * P].rearrange("l (c p) n -> p (l c) n", p=P)).then_inc(ffn_w_in, 16)
                sp.dma_start(w2[0:F - 2 * P, 2, :], f_w2[bass.ds(L, 1), 2 * P:F].rearrange("l p n -> p (l n)")).then_inc(ffn_w_in, 16)
                sp.dma_start(lng[:], f_g[bass.ds(L, 1)].rearrange("l p -> p l")).then_inc(ffn_w_in, 16)
                sp.dma_start(lnb[:], f_b[bass.ds(L, 1)].rearrange("l p -> p l")).then_inc(ffn_w_in, 16)
                sp.dma_start(b1r[:], f_b1[bass.ds(L, 1)].to_broadcast([P, 2 * F])).then_inc(ffn_w_in, 16)
                sp.dma_start(b2r[:], f_b2[bass.ds(L, 1)].to_broadcast([P, D])).then_inc(ffn_w_in, 16)
                with sp.Fori(0, B) as j:
                    sp.wait_ge(v_done, (L * AT + j * 2) * 2 + (2 + CR))
                    sp.wait_ge(pv_done, (L * NT + j * 2) * PAIRS + CR)
                    sp.dma_start(vt[:], v[P - WIN:P, 0, :]).then_inc(vtail_done, 16)
            for i in range(4):
                part = slice(i * NT // 4, (i + 1) * NT // 4)
                sp.wait_ge(gated, i + 1)
                sp.dma_start(o_dram[:, part, :], x[:, part, :]).then_inc(out_done, 16)
            sp.wait_ge(out_done, 64)

        @block.gpsimd
        def _(pool):
            for s in (xs_ready, rsum_done, guard_done, rn_done, rot_done, f_var, f_rstd, f_hm):
                pool.sem_inc(s, CR)
            nc.gpsimd.memset(neg_half[:], -0.5).then_inc(pool_setup, 1)
            nc.gpsimd.memset(eps[:], EPS).then_inc(pool_setup, 1)
            nc.gpsimd.memset(x[:, NT, :], 0.0).then_inc(pool_setup, 1)
            nc.gpsimd.memset(yTf[:, :, 0:1], 0.0).then_inc(pool_setup, 1)
            nc.gpsimd.memset(yT[:, 0:1], 0.0).then_inc(pool_setup, 1)
            pool.wait_ge(pool_setup, 5)
            nc.gpsimd.memset(qT[0:DH, :, 1], 0.0).then_inc(pool_setup, 1)
            pool.wait_ge(pool_setup, 6)
            nc.gpsimd.memset(qT[DH:P, :, 0], 0.0).then_inc(pool_setup, 1)
            pool.wait_ge(pool_setup, POOL_SETUP)

            with pool.Fori(0, B) as b:
                for half in range(2):
                    pool.wait_ge(m_act, b * AA + (3, AA)[half])
                    nc.gpsimd.tensor_tensor(var1[:], ssq[:], eps[:, 0:TPB], ALU.add).then_inc(m_pool, 1)
                    pool.wait_ge(m_pool, b * GA + (2 * half + 1))
                    nc.gpsimd.tensor_tensor(rstd[:], var1[:], neg_half[:, 0:TPB], ALU.pow).then_inc(m_pool, 1)

            def load_x(tile):
                nc.gpsimd.tensor_copy(xs[:], x[:, tile, :].rearrange("p a d -> p (a d)")).then_inc(xs_ready, 1)

            def rotate(a):
                for c in range(KQ):
                    n = a * KQ + c
                    slot = c % 2
                    pool.wait_ge(prod_done, n + (1 + CR))
                    nc.gpsimd.tensor_tensor(rsum[:, slot, :], rc[:, slot, :], rs[:, slot, :], ALU.add).then_inc(rsum_done, 1)
                    settle(pool)
                    pool.wait_ge(red_done, n + (1 + CR))
                    nc.gpsimd.tensor_scalar(n2g[:, c, :], n2[:, c, :], 1e-24, None, ALU.max).then_inc(guard_done, 1)
                    pool.wait_ge(guard_done, n + (1 + CR))
                    nc.gpsimd.tensor_tensor(rn[:, c, :], n2g[:, c, :], neg_half[:], ALU.pow).then_inc(rn_done, 1)
                    pool.wait_ge(rn_done, n + (1 + CR))
                    pool.wait_ge(rot_turned, n + (CR - 1))
                    nc.gpsimd.tensor_tensor(
                        rot[:, slot, :].rearrange("p (h d) -> p h d", d=DH),
                        rsum[:, slot, :].rearrange("p (h d) -> p h d", d=DH),
                        rn[:, c, :, None].to_broadcast([P, HPC, DH]), ALU.mult).then_inc(rot_done, 1)

            with pool.Fori(0, DEPTH) as L:
                pool.wait_ge(attn_w_in, (L + 1) * (16 * N_ATTN))
                pool.wait_ge(x_full, (L + 1) * B)
                for i in range(4):
                    s = scales[:, i // 2, :].rearrange("p (x d) -> p x d", x=2)
                    if i % 2:
                        s = s[:, ::-1, :]
                    for t in range(TPB):
                        nc.gpsimd.tensor_tensor(
                            tables[:, i, t, :].rearrange("p (x d) -> p x d", x=2),
                            rope[:, i, t, :].rearrange("p (x d) -> p x d", x=2), s, ALU.mult).then_inc(tables_done, 1)
                load_x(bass.ds(0, 1))
                rotate(L * AT)
                with pool.Fori(0, B) as j:
                    load_x(bass.ds(j * 2 + 1, 1))
                    rotate(L * AT + j * 2 + 1)
                    load_x(bass.ds(j * 2 + 2, 1))
                    rotate(L * AT + j * 2 + 2)
                with pool.Fori(0, NF) as f:
                    k = L * NF + f
                    pool.wait_ge(f_ss, k * FT + (FT + CR))
                    nc.gpsimd.tensor_tensor(vaf[:], ssf[:], eps[:, 0:FT], ALU.add).then_inc(f_var, 1)
                    pool.wait_ge(f_var, k + (1 + CR))
                    nc.gpsimd.tensor_tensor(rsf[:], vaf[:], neg_half[:, 0:FT], ALU.pow).then_inc(f_rstd, 1)
                    for i in range(FT):
                        n = k * FT + i
                        pool.wait_ge(f_gelu, n + (1 + CR))
                        pool.wait_ge(f_hT, n + (CR - 1))
                        nc.gpsimd.tensor_tensor(hm[:, i % 2, :], ha[:, i % 2, :], gg[:, i % 2, :], ALU.mult).then_inc(f_hm, 1)

        @block.scalar
        def _(act):
            for s in (yT_ready, sq_done, t_copied, ktail_done, v_done, exp_done, pt_copied, o_copied,
                      w1c_done, f_yT, f_ss, f_gelu, f_hTc):
                act.sem_inc(s, CR)
            act.wait_ge(dve_setup, 11)
            nc.scalar.activation(csig[:], cT[:], ACT.Exp, scale=-1.0).then_inc(act_setup, 1)

            with act.Fori(0, B) as b:
                act.wait_ge(m_pe, b * PA + 1)
                nc.scalar.activation(mod[:, 0:3, :], bank[0][:, 0:3 * D].rearrange("p (a d) -> p a d", d=D), ACT.Copy)
                nc.scalar.activation(mod[:, 3:6, :], bank[1][:, 0:3 * D].rearrange("p (a d) -> p a d", d=D), ACT.Copy).then_inc(m_act, 1)
                act.wait_ge(m_dve, b * DA + 4)
                nc.scalar.activation(sqj[:, 0, :], xc[:, 0, :], ACT.Square, scale=RMS_SCALE, accum_out=ssq[:, 0:1]).then_inc(m_act, 1)
                nc.scalar.activation(sqj[:, 1, :], xc[:, 1, :], ACT.Square, scale=RMS_SCALE, accum_out=ssq[:, 1:2]).then_inc(m_act, 1)
                act.wait_ge(m_pe, b * PA + 2)
                nc.scalar.activation(h1T[:], bank[2][:, 0:S], ACT.Copy).then_inc(m_act, 1)
                act.wait_ge(m_pe, b * PA + 3)
                nc.scalar.activation(q1T[:], bank[3][:, 0:S], ACT.Copy).then_inc(m_act, 1)
                nc.scalar.activation(k1T[:], bank[4][:, 0:S], ACT.Copy).then_inc(m_act, 1)
                act.wait_ge(m_dve, b * DA + 16)
                nc.scalar.activation(p1[:, 0:P], bank[6][:, 0:P], ACT.Exp, scale=ATT1_SCALE, bias=nms1[:, 0:1],
                                     accum_out=sum1[:, 0:1]).then_inc(m_act, 1)
                nc.scalar.activation(p1[:, P:P + S], bank[6][:, P:P + S], ACT.Exp, scale=ATT1_SCALE, bias=nms1[:, 1:2],
                                     accum_out=sum1[:, 1:2]).then_inc(m_act, 1)
                act.wait_ge(m_pe, b * PA + 5)
                nc.scalar.activation(p1T[:], bank[7][:, 0:3 * P], ACT.Copy).then_inc(m_act, 1)
                act.wait_ge(m_pe, b * PA + 6)
                nc.scalar.activation(o1T[:], bank[0][:, 0:S], ACT.Copy).then_inc(m_act, 1)
                act.wait_ge(m_dve, b * DA + 24)
                nc.scalar.activation(sqj[:, 0, :], xc[:, 0, :], ACT.Square, scale=RMS_SCALE, accum_out=ssq[:, 0:1]).then_inc(m_act, 1)
                nc.scalar.activation(sqj[:, 1, :], xc[:, 1, :], ACT.Square, scale=RMS_SCALE, accum_out=ssq[:, 1:2]).then_inc(m_act, 1)

            def exps(g, s, N):
                act.wait_ge(max_done, g + (s + 1 + CR))
                act.wait_ge(pt_done, g + (s - 1 + CR))
                slot = s % 2
                for h in range(2):
                    last = nc.scalar.activation(pr[:, slot, h, 0:N], SIM[slot][:, h * N:(h + 1) * N], ACT.Exp,
                                                bias=nmax[:, slot, h:h + 1], accum_out=psm[:, slot, h:h + 1])
                last.then_inc(exp_done, 1)

            def pt_copy(g, s, par):
                act.wait_ge(pt_done, g + (s + 1 + CR))
                act.wait_ge(pv_done, g + (s - 1 + CR))
                n = 2 * P + (2 * WIN if par else 0)
                nc.scalar.activation(pT[:, s % 2, 0:n], PT[:, 0:n], ACT.Copy).then_inc(pt_copied, 1)

            def o_copy(b, half):
                act.wait_ge(pv_done, b * PAIRS + (4 * half + 4 + CR))
                act.wait_ge(wo_done, b + CR)
                nc.scalar.activation(oT[:, 4 * half:4 * half + 4, :], O[:].rearrange("p (c t) -> p c t", c=4),
                                     ACT.Copy).then_inc(o_copied, 1)

            def y_copy(a, par):
                act.wait_ge(xT_done, a + (1 + CR))
                nc.scalar.activation(yT[0:64, par * P:(par + 1) * P], T[0:64, 0:P], ACT.Copy)
                nc.scalar.activation(yT[64:P, par * P + 1:(par + 1) * P + 1], T[64:P, 0:P], ACT.Copy).then_inc(yT_ready, 1)

            def square(a, c):
                act.wait_ge(chunk_done, a * 6 + (c + 1 + CR))
                act.wait_ge(red_done, a * KQ + (c - 1 + CR))
                nc.scalar.activation(sq[:, c % 2, :], G[c % 2][:], ACT.Square).then_inc(sq_done, 1)

            def t_copy(a, c, par):
                act.wait_ge(rot_turned, a * KQ + (c + 1 + CR))
                half = slice(4 * (c % 2), 4 * (c % 2) + 4)
                src = T[:].rearrange("p (c t) -> p c t", c=4)
                if c >= 2:
                    nc.scalar.activation(qT[0:DH, par, 0, half, :], src[0:DH], ACT.Copy)
                    nc.scalar.activation(qT[DH:P, par, 1, half, :], src[DH:P], ACT.Copy).then_inc(t_copied, 1)
                    return
                if par:
                    dst = kTo[:, half, WIN:WIDE]
                else:
                    dst = kTe[:, half, :]
                nc.scalar.activation(dst, src, ACT.Copy).then_inc(t_copied, 1)

            def v_copy(a, c, par):
                act.wait_ge(chunk_done, a * 6 + (KQ + c + 1 + CR))
                nc.scalar.activation(v[:, par, c * CH:(c + 1) * CH], G[c % 2][:], ACT.Copy).then_inc(v_done, 1)

            def tile(b, a, par, batch):
                g = b * PAIRS
                N = WIDE if par else P
                nxt = 1 - par
                y_copy(a, nxt)
                exps(g, 0, N)
                for s in range(PAIRS):
                    if s + 1 < PAIRS:
                        exps(g, s + 1, N)
                    pt_copy(g, s, par)
                    if s < KQ:
                        square(a, s)
                    if s == 3 and nxt:
                        act.wait_ge(sims_done, g + (1 + CR))
                        nc.scalar.activation(kTo[:, :, 0:WIN], kTe[:, :, P - WIN:P], ACT.Copy).then_inc(ktail_done, 1)
                    if s == 5:
                        o_copy(b, 0)
                        if not nxt:
                            act.wait_ge(vtail_done, batch * 16 + 16)
                        v_copy(a, 0, nxt)
                    if s >= KQ:
                        t_copy(a, s - KQ, nxt)
                o_copy(b, 1)
                v_copy(a, 1, nxt)

            with act.Fori(0, DEPTH) as L:
                y_copy(L * AT, 0)
                for c in range(KQ):
                    square(L * AT, c)
                for c in range(KQ):
                    t_copy(L * AT, c, 0)
                for c in range(2):
                    v_copy(L * AT, c, 0)
                with act.Fori(0, B) as j:
                    for par in range(2):
                        tile(L * NT + j * 2 + par, L * AT + j * 2 + par + 1, par, L * B + j)
                act.wait_ge(w1c_mm, L + (1 + CR))
                nc.scalar.activation(w1c[:, 0:F], bank[0][:, 0:F], ACT.Copy)
                nc.scalar.activation(w1c[:, F:2 * F], bank[1][:, 0:F], ACT.Copy).then_inc(w1c_done, 1)
                with act.Fori(0, NF) as f:
                    k = L * NF + f
                    act.wait_ge(f_xT, k + (1 + CR))
                    turned = FT_B[:].rearrange("p (b t) -> p b t", b=FT // TPB)
                    nc.scalar.activation(yTf[0:64, :, 0:S], turned[0:64], ACT.Copy)
                    nc.scalar.activation(yTf[64:P, :, 1:S + 1], turned[64:P], ACT.Copy).then_inc(f_yT, 1)
                    act.wait_ge(f_yc, k + (1 + CR))
                    for i in range(FT):
                        nc.scalar.activation(sqf[:, i, :], FYC[:, i * P:(i + 1) * P], ACT.Square, scale=RMS_SCALE,
                                             accum_out=ssf[:, i:i + 1]).then_inc(f_ss, 1)
                    for i in range(FT + 1):
                        n = k * FT + i
                        if i < FT:
                            act.wait_ge(f_hb, n + (1 + CR))
                            act.wait_ge(f_hm, n + (CR - 1))
                            nc.scalar.activation(gg[:, i % 2, :], hg[:, i % 2, :], ACT.Gelu).then_inc(f_gelu, 1)
                        if i >= 1:
                            act.wait_ge(f_hT, n + CR)
                            nc.scalar.activation(hT[:, (i - 1) % 2, :], FHT[:, 0:3 * P], ACT.Copy).then_inc(f_hTc, 1)

        @block.vector
        def _(dve):
            for s in (red_done, prod_done, max_done, inv_done, norm_done, x_upd, w1g_done, bias_done, f_xs, f_hb):
                dve.sem_inc(s, CR)
            for i in range(8):
                nc.vector.memset(bank[i][:], 0.0).then_inc(dve_setup, 1)
            dve.wait_ge(const_in, 16 * N_CONST)
            nc.vector.tensor_copy(identb[:], ident[:]).then_inc(dve_setup, 1)
            nc.vector.tensor_copy(masks[:], mask_f[:]).then_inc(dve_setup, 1)
            dve.wait_ge(pe_setup, 1)
            nc.vector.tensor_copy(cT[:], bank[0][:, 0:B]).then_inc(dve_setup, 1)
            dve.wait_ge(act_setup, 1)
            nc.vector.tensor_scalar(cden[:], csig[:], 1.0, None, ALU.add).then_inc(dve_setup, 1)
            dve.wait_ge(dve_setup, 12)
            nc.vector.reciprocal(cinv[:], cden[:]).then_inc(dve_setup, 1)
            dve.wait_ge(dve_setup, 13)
            nc.vector.tensor_tensor(csilu[:], cT[:], cinv[:], ALU.mult).then_inc(dve_setup, 1)
            dve.wait_ge(dve_setup, 14)

            with dve.Fori(0, B) as b:
                tiles = bass.ds(b * TPB, TPB)
                at = b * DA

                def centred(first, src):
                    nc.vector.tensor_reduce(tsum[:], src, AX.X, ALU.add).then_inc(m_dve, 1)
                    dve.wait_ge(m_dve, at + first)
                    nc.vector.tensor_scalar(nmean[:], tsum[:], -1.0 / D, None, ALU.mult).then_inc(m_dve, 1)
                    dve.wait_ge(m_dve, at + (first + 1))
                    nc.vector.tensor_tensor(xc[:], src, nmean[:, :, None].to_broadcast([P, TPB, D]),
                                            ALU.add).then_inc(m_dve, 1)

                nc.vector.tensor_copy(cb_l[:], csilu[:, bass.ds(b, 1)].to_broadcast([P, P])).then_inc(m_dve, 1)
                centred(2, x1[:, tiles, :])
                dve.wait_ge(m_act, b * AA + 1)
                nc.vector.tensor_scalar(mod[:, 1::3, :], mod[:, 1::3, :], 1.0, None, ALU.add)
                nc.vector.tensor_scalar(gate_pos[:], mod[:, 2::3, :], 0.25, None, ALU.max).then_inc(m_dve, 1)
                nc.vector.tensor_scalar(gate_sign[:], mod[:, 2::3, :], 0.0, 2.0, ALU.is_ge, ALU.mult).then_inc(m_dve, 1)
                dve.wait_ge(m_dve, at + 5)
                nc.vector.scalar_tensor_tensor(out=gate_abs[:], in0=mod[:, 2::3, :], scalar=-1.0, in1=gate_pos[:],
                                               op0=ALU.mult, op1=ALU.max).then_inc(m_dve, 1)
                dve.wait_ge(m_dve, at + 7)
                nc.vector.scalar_tensor_tensor(out=ga[:], in0=gate_sign[:, 0, :], scalar=-1.0, in1=gate_abs[:, 0, :],
                                               op0=ALU.add, op1=ALU.mult).then_inc(m_dve, 1)
                nc.vector.scalar_tensor_tensor(out=gb[:, bass.ds(b, 1), :].rearrange("p a d -> p (a d)"), in0=gate_sign[:, 1, :],
                                               scalar=-1.0, in1=gate_abs[:, 1, :], op0=ALU.add, op1=ALU.mult).then_inc(m_dve, 1)
                dve.wait_ge(m_pool, b * GA + 2)
                for t in range(TPB):
                    nc.vector.scalar_tensor_tensor(out=h1[:, t, :], in0=xc[:, t, :], scalar=rstd[:, t:t + 1], in1=mod[:, 1, :],
                                                   op0=ALU.mult, op1=ALU.mult).then_inc(m_dve, 1)
                dve.wait_ge(m_dve, at + 11)
                nc.vector.tensor_tensor(h1s[:], h1[:], mod[:, 0:1, :].to_broadcast([P, TPB, D]), ALU.add).then_inc(m_dve, 1)
                dve.wait_ge(m_pe, b * PA + 3)
                nc.vector.tensor_copy(v1[:], bank[5][:, 0:S].rearrange("p (t d) -> p t d", t=TPB)).then_inc(m_dve, 1)
                dve.wait_ge(m_pe, b * PA + 4)
                nc.vector.tensor_reduce(nm1[:, 0:1], bank[6][:, 0:P], AX.X, ALU.max, negate=True).then_inc(m_dve, 1)
                nc.vector.tensor_reduce(nm1[:, 1:2], bank[6][:, P:P + S], AX.X, ALU.max, negate=True).then_inc(m_dve, 1)
                dve.wait_ge(m_dve, at + 15)
                nc.vector.tensor_scalar(nms1[:], nm1[:], ATT1_SCALE, None, ALU.mult).then_inc(m_dve, 1)
                dve.wait_ge(m_act, b * AA + 8)
                nc.vector.reciprocal(rin1[:], sum1[:]).then_inc(m_dve, 1)
                dve.wait_ge(m_dve, at + 17)
                nc.vector.tensor_scalar(p1[:, 0:P], p1[:, 0:P], rin1[:, 0:1], None, ALU.mult).then_inc(m_dve, 1)
                nc.vector.tensor_scalar(p1[:, P:P + S], p1[:, P:P + S], rin1[:, 1:2], None, ALU.mult).then_inc(m_dve, 1)
                dve.wait_ge(m_pe, b * PA + 7)
                nc.vector.tensor_tensor(att1[:], bank[1][:, 0:S].rearrange("p (t d) -> p t d", t=TPB),
                                        ga[:, None, :].to_broadcast([P, TPB, D]), ALU.mult).then_inc(m_dve, 1)
                dve.wait_ge(m_dve, at + 20)
                nc.vector.tensor_tensor(xn[:], x1[:, tiles, :], att1[:], ALU.add).then_inc(m_dve, 1)
                dve.wait_ge(m_dve, at + 21)
                centred(22, xn[:])
                nc.vector.tensor_copy(x1[:, tiles, :], xn[:])
                dve.wait_ge(m_pool, b * GA + 4)
                for t in range(TPB):
                    nc.vector.scalar_tensor_tensor(out=h1[:, t, :], in0=xc[:, t, :], scalar=rstd[:, t:t + 1], in1=mod[:, 4, :],
                                                   op0=ALU.mult, op1=ALU.mult).then_inc(m_dve, 1)
                dve.wait_ge(m_dve, at + 26)
                nc.vector.tensor_tensor(x[:, tiles, :], h1[:], mod[:, 3:4, :].to_broadcast([P, TPB, D]), ALU.add).then_inc(x_full, 1)

            def products(a, c, par):
                dve.wait_ge(sq_done, a * KQ + (c + 1 + CR))
                dve.wait_ge(rsum_done, a * KQ + (c - 1 + CR))
                slot, which = c % 2, 2 * (c // 2)
                nc.vector.tensor_tensor(rc[:, slot, :].rearrange("p (h d) -> p h d", d=DH),
                                        G[slot][:].rearrange("p (h d) -> p h d", d=DH),
                                        tables[:, which, par:par + 1, :].to_broadcast([P, HPC, DH]), ALU.mult)
                nc.vector.tensor_tensor(
                    rs[:, slot, :].rearrange("p (h x d) -> p h x d", x=2, d=DH // 2),
                    G[slot][:].rearrange("p (h x d) -> p h x d", x=2, d=DH // 2)[:, :, ::-1, :],
                    tables[:, which + 1, par:par + 1, :].to_broadcast([P, HPC, DH]).rearrange("p h (x d) -> p h x d", x=2),
                    ALU.mult).then_inc(prod_done, 1)

            def norms(a, c):
                dve.wait_ge(sq_done, a * KQ + (c + 1 + CR))
                nc.vector.tensor_reduce(n2[:, c, :], sq[:, c % 2, :].rearrange("p (h d) -> p h d", d=DH), AX.X,
                                        ALU.add).then_inc(red_done, 1)

            def maxima(g, s, N):
                dve.wait_ge(sims_done, g + (s + 1 + CR))
                nc.vector.tensor_reduce(nmax[:, s % 2, :], SIM[s % 2][:, 0:2 * N].rearrange("p (h n) -> p h n", h=2), AX.X,
                                        ALU.max, negate=True).then_inc(max_done, 1)

            def normalise(g, s, N):
                slot = s % 2
                dve.wait_ge(exp_done, g + (s + 1 + CR))
                nc.vector.reciprocal(pinv[:, slot, :], psm[:, slot, :]).then_inc(inv_done, 1)
                dve.wait_ge(inv_done, g + (s + 1 + CR))
                for h in range(2):
                    last = nc.vector.tensor_scalar(pr[:, slot, h, 0:N], pr[:, slot, h, 0:N], pinv[:, slot, h:h + 1], None, ALU.mult)
                last.then_inc(norm_done, 1)

            def tile(b, a, par, at_tile):
                g = b * PAIRS
                N = WIDE if par else P
                nxt = 1 - par
                maxima(g, 0, N)
                maxima(g, 1, N)
                for s in range(PAIRS):
                    normalise(g, s, N)
                    if s + 2 < PAIRS:
                        maxima(g, s + 2, N)
                    if s < KQ:
                        products(a, s, nxt)
                    if 1 <= s <= KQ:
                        norms(a, s - 1)
                dve.wait_ge(wo_done, b + (1 + CR))
                xt = x[:, at_tile, :].rearrange("p a d -> p (a d)")
                nc.vector.tensor_tensor(xt, Z[:, 0:D], xt, ALU.add).then_inc(x_upd, 1)

            with dve.Fori(0, DEPTH) as L:
                dve.wait_ge(tables_done, L * 8 + 8)
                for c in range(KQ):
                    products(L * AT, c, 0)
                    norms(L * AT, c)
                with dve.Fori(0, B) as j:
                    for par in range(2):
                        tile(L * NT + j * 2 + par, L * AT + j * 2 + par + 1, par, bass.ds(j * 2 + par, 1))
                dve.wait_ge(ffn_w_in, (L + 1) * (16 * N_FFN))
                nc.vector.tensor_scalar(w1g[:], w1[:], lng[:, 0:1], None, ALU.mult)
                nc.vector.tensor_copy(lnb_l[:], lnb[:, 0:1].to_broadcast([P, P])).then_inc(w1g_done, 1)
                dve.wait_ge(x_upd, (L + 1) * NT + CR)
                dve.wait_ge(bias_mm, L + (1 + CR))
                nc.vector.tensor_tensor(bias1[:, 0:F], bank[5][:, 0:F], b1r[:, 0:F], ALU.add)
                nc.vector.tensor_tensor(bias1[:, F:2 * F], bank[6][:, 0:F], b1r[:, F:2 * F], ALU.add).then_inc(bias_done, 1)
                with dve.Fori(0, NF) as f:
                    k = L * NF + f
                    dve.wait_ge(x_full, L * B + f * 2 + B)
                    nc.vector.tensor_tensor(xbf[:], x[:, bass.ds(f * FT, FT), :],
                                            b2r[:, None, :].to_broadcast([P, FT, D]), ALU.add)
                    nc.vector.tensor_copy(xsf[:], x[:, bass.ds(f * FT, FT), :]).then_inc(f_xs, 1)
                    dve.wait_ge(f_rstd, k + (1 + CR))
                    for i in range(FT):
                        n = k * FT + i
                        dve.wait_ge(f_h, n + (1 + CR))
                        dve.wait_ge(f_hm, n + (CR - 1))
                        ba, bg = FH[i % 2]
                        nc.vector.scalar_tensor_tensor(out=ha[:, i % 2, :], in0=ba[:, 0:F], scalar=rsf[:, i:i + 1],
                                                       in1=bias1[:, 0:F], op0=ALU.mult, op1=ALU.add)
                        nc.vector.scalar_tensor_tensor(out=hg[:, i % 2, :], in0=bg[:, 0:F], scalar=rsf[:, i:i + 1],
                                                       in1=bias1[:, F:2 * F], op0=ALU.mult, op1=ALU.add).then_inc(f_hb, 1)
                    dve.wait_ge(f_z, k + (1 + CR))
                    dve.wait_ge(f_xs, k + (1 + CR))
                    nc.vector.tensor_tensor(x[:, bass.ds(f * FT, FT), :], FZ[:].rearrange("p (t d) -> p t d", t=FT), xbf[:],
                                            ALU.add).then_inc(x_full, 2)
            dve.wait_ge(x_full, (DEPTH + 1) * B)
            for i in range(4):
                part = slice(i * NT // 4, (i + 1) * NT // 4)
                xv = x[:, part, :].rearrange("p (b t) d -> p b t d", t=TPB)
                nc.vector.tensor_tensor(xv, xv, gb[:, i * B // 4:(i + 1) * B // 4, None, :].to_broadcast([P, B // 4, TPB, D]),
                                        ALU.mult).then_inc(scaled, 1)
            for i in range(4):
                part = slice(i * NT // 4, (i + 1) * NT // 4)
                dve.wait_ge(scaled, i + 1)
                nc.vector.tensor_tensor(x[:, part, :], x[:, part, :], x1[:, part, :], ALU.add).then_inc(gated, 1)

        @block.tensor
        def _(pe):
            for s in (xT_done, chunk_done, rot_turned, sims_done, pt_done, pv_done, wo_done,
                      w1c_mm, bias_mm, f_xT, f_yc, f_h, f_hT, f_z):
                pe.sem_inc(s, CR)
            mm = nc.tensor.matmul
            pe.wait_ge(const_in, 16 * N_CONST)
            pe.wait_ge(dve_setup, 10)
            nc.tensor.transpose(bank[0][:, 0:B], crow[:], ident[0:B, 0:B]).then_inc(pe_setup, 1)

            with pe.Fori(0, B) as b:
                pe.wait_ge(m_dve, b * DA + 1)
                mm(bank[0][:, 0:3 * D], cb_l[:], wmod_s[:, 0:3 * D], start=True, stop=True)
                mm(bank[1][:, 0:3 * D], cb_l[:], wmod_s[:, 3 * D:6 * D], start=True, stop=True).then_inc(m_pe, 1)
                pe.wait_ge(m_dve, b * DA + 12)
                for t in range(TPB):
                    last = nc.tensor.transpose(bank[2][:, t * P:(t + 1) * P], h1s[:, t, :], ident[:])
                last.then_inc(m_pe, 1)
                pe.wait_ge(m_act, b * AA + 4)
                mm(bank[3][:, 0:S], w1q[:], h1T[:], start=True, stop=True)
                mm(bank[4][:, 0:S], w1k[:], h1T[:], start=True, stop=True)
                for t in range(TPB):
                    last = mm(bank[5][:, t * D:(t + 1) * D], h1T[:, t * P:(t + 1) * P], w1v[:], start=True, stop=True)
                last.then_inc(m_pe, 1)
                pe.wait_ge(m_act, b * AA + 6)
                for q, k, at in ((0, 0, 0), (1, 0, 1), (1, 1, 2)):
                    o = bank[6][:, at * P:(at + 1) * P]
                    if q == k:
                        mm(o, identb[:], mask_causal, start=True, stop=False)
                    last = mm(o, q1T[:, q * P:(q + 1) * P], k1T[:, k * P:(k + 1) * P], start=(q != k), stop=True)
                last.then_inc(m_pe, 1)
                pe.wait_ge(m_dve, b * DA + 19)
                for i in range(3):
                    last = nc.tensor.transpose(bank[7][:, i * P:(i + 1) * P], p1[:, i * P:(i + 1) * P], ident[:])
                last.then_inc(m_pe, 1)
                pe.wait_ge(m_act, b * AA + 9)
                mm(bank[0][:, 0:P], v1[:, 0, :], p1T[:, 0:P], start=True, stop=True)
                mm(bank[0][:, P:S], v1[:, 0, :], p1T[:, P:2 * P], start=True, stop=False)
                mm(bank[0][:, P:S], v1[:, 1, :], p1T[:, 2 * P:3 * P], start=False, stop=True).then_inc(m_pe, 1)
                pe.wait_ge(m_act, b * AA + 10)
                for t in range(TPB):
                    last = mm(bank[1][:, t * D:(t + 1) * D], o1T[:, t * P:(t + 1) * P], w1o[:], start=True, stop=True)
                last.then_inc(m_pe, 1)

            def x_turn(a):
                pe.wait_ge(xs_ready, a + (1 + CR))
                pe.wait_ge(t_copied, a * KQ + CR)
                nc.tensor.transpose(T[:, 0:P], xs[:], ident[:]).then_inc(xT_done, 1)

            def chunk(a, c, par):
                if c == 0:
                    pe.wait_ge(yT_ready, a + (1 + CR))
                if c < 2:
                    pe.wait_ge(v_done, a * 2 + (c - 1 + CR))
                else:
                    pe.wait_ge(prod_done, a * KQ + (c - 1 + CR))
                mm(G[c % 2][:], yT[:, par * P:(par + 1) * P], wqkv[:, CHUNK_COL[c]:CHUNK_COL[c] + CH],
                   start=True, stop=True).then_inc(chunk_done, 1)

            def turn(a, c):
                pe.wait_ge(rot_done, a * KQ + (c + 1 + CR))
                pe.wait_ge(t_copied, a * KQ + (c + CR))
                for i in range(4):
                    last = nc.tensor.transpose(T[:, i * P:(i + 1) * P], rot[:, c % 2, i * P:(i + 1) * P], ident[:])
                last.then_inc(rot_turned, 1)

            def sims(g, a, s, par, batch):
                if s == 0:
                    pe.wait_ge(t_copied, a * KQ + (3 + CR))
                    if par:
                        pe.wait_ge(ktail_done, batch + (1 + CR))
                if s == 4:
                    pe.wait_ge(t_copied, a * KQ + (4 + CR))
                pe.wait_ge(exp_done, g + (s - 1 + CR))
                N = WIDE if par else P
                kT, mask = (kTo, mask_odd) if par else (kTe, mask_even)
                bk = SIM[s % 2]
                mm(bk[:, 0:2 * N].rearrange("p (h n) -> p h n", h=2), identb[:], mask[:, None, :].to_broadcast([P, 2, N]),
                   start=True, stop=False, skip_group_check=True)
                for h in range(2):
                    last = mm(bk[:, h * N:(h + 1) * N], qT[:, par, h, s, :], kT[:, s, :], start=False, stop=(h == 1),
                              skip_group_check=True)
                last.then_inc(sims_done, 1)

            def p_turn(g, s, par):
                pe.wait_ge(norm_done, g + (s + 1 + CR))
                pe.wait_ge(pt_copied, g + (s + CR))
                slot = s % 2
                own = WIN if par else 0
                for h in range(2):
                    last = nc.tensor.transpose(PT[:, h * P:(h + 1) * P], pr[:, slot, h, own:own + P], ident[:])
                if par:
                    for h in range(2):
                        last = nc.tensor.transpose(PT[0:WIN, 2 * P + h * WIN:2 * P + (h + 1) * WIN], pr[0:WIN, slot, h, 0:WIN],
                                                   ident[0:WIN, 0:WIN])
                last.then_inc(pt_done, 1)

            def outputs(b, g, a, s, par, batch):
                pe.wait_ge(pt_copied, g + (s + 1 + CR))
                if s == 0:
                    pe.wait_ge(v_done, a * 2 + (1 + CR))
                    if par:
                        pe.wait_ge(vtail_done, batch * 16 + 16)
                if s == 4:
                    pe.wait_ge(v_done, a * 2 + (2 + CR))
                if s % 4 == 0:
                    pe.wait_ge(o_copied, b * 2 + (s // 4 + CR))
                slot, col = s % 2, (s % 4) * P
                for h in range(2):
                    head = slice((2 * s + h) * DH, (2 * s + h + 1) * DH)
                    half = slice(h * DH, (h + 1) * DH)
                    last = mm(O[half, col:col + P], v[:, par, head], pT[:, slot, h * P:(h + 1) * P], start=True, stop=not par,
                              skip_group_check=True)
                    if par:
                        last = mm(O[half, col:col + WIN], vt[:, head], pT[0:WIN, slot, 2 * P + h * WIN:2 * P + (h + 1) * WIN],
                                  start=False, stop=True, skip_group_check=True)
                last.then_inc(pv_done, 1)

            def tile(b, a, par, batch):
                g = b * PAIRS
                nxt = 1 - par
                x_turn(a)
                sims(g, a - 1, 0, par, batch)
                sims(g, a - 1, 1, par, batch)
                for s in range(PAIRS):
                    p_turn(g, s, par)
                    if s + 2 < PAIRS:
                        sims(g, a - 1, s + 2, par, batch)
                    if s < KQ:
                        chunk(a, s, nxt)
                    if s == 5:
                        chunk(a, 4, nxt)
                    if s >= KQ:
                        turn(a, s - KQ)
                    if s >= 1:
                        outputs(b, g, a - 1, s - 1, par, batch)
                outputs(b, g, a - 1, PAIRS - 1, par, batch)
                chunk(a, 5, nxt)
                pe.wait_ge(o_copied, b * 2 + (2 + CR))
                pe.wait_ge(x_upd, b + CR)
                for c in range(PAIRS):
                    last = mm(Z[:, 0:D], oT[:, c, :], wo[:, c, :], start=(c == 0), stop=(c == PAIRS - 1))
                last.then_inc(wo_done, 1)

            with pe.Fori(0, DEPTH) as L:
                pe.wait_ge(x_full, (L + 1) * B)
                pe.wait_ge(attn_w_in, (L + 1) * (16 * N_ATTN))
                x_turn(L * AT)
                for c in range(6):
                    chunk(L * AT, c, 0)
                for c in range(KQ):
                    turn(L * AT, c)
                with pe.Fori(0, B) as j:
                    for par in range(2):
                        tile(L * NT + j * 2 + par, L * AT + j * 2 + par + 1, par, L * B + j)
                pe.wait_ge(x_upd, (L + 1) * NT + CR)
                pe.wait_ge(v_done, (L + 1) * (2 * AT) + CR)
                pe.wait_ge(t_copied, (L + 1) * (KQ * AT) + CR)
                pe.wait_ge(w1g_done, L + (1 + CR))
                for i in range(2):
                    last = mm(bank[i][:, 0:F], center[:], w1g[:, i * F:(i + 1) * F], start=True, stop=True)
                last.then_inc(w1c_mm, 1)
                for i in range(2):
                    last = mm(bank[5 + i][:, 0:F], lnb_l[:], w1[:, i * F:(i + 1) * F], start=True, stop=True)
                last.then_inc(bias_mm, 1)
                with pe.Fori(0, NF) as f:
                    k = L * NF + f
                    pe.wait_ge(f_xs, k + (1 + CR))
                    for i in range(FT):
                        last = nc.tensor.transpose(FT_B[:, i * P:(i + 1) * P], xsf[:, i, :], ident[:])
                    last.then_inc(f_xT, 1)
                    pe.wait_ge(f_yT, k + (1 + CR))
                    pe.wait_ge(f_ss, k * FT + CR)
                    for i in range(FT):
                        last = mm(FYC[:, i * P:(i + 1) * P], yTf[:, i // TPB, (i % TPB) * P:(i % TPB + 1) * P], center[:],
                                  start=True, stop=True)
                    last.then_inc(f_yc, 1)

                    def hidden(i):
                        pe.wait_ge(f_hb, k * FT + (i - 1 + CR))
                        for half in range(2):
                            last = mm(FH[i % 2][half][:, 0:F], yTf[:, i // TPB, (i % TPB) * P:(i % TPB + 1) * P],
                                      w1c[:, half * F:(half + 1) * F], start=True, stop=True)
                        last.then_inc(f_h, 1)

                    pe.wait_ge(w1c_done, L + (1 + CR))
                    pe.wait_ge(bias_done, L + (1 + CR))
                    hidden(0)
                    hidden(1)
                    for i in range(FT):
                        n = k * FT + i
                        pe.wait_ge(f_hm, n + (1 + CR))
                        pe.wait_ge(f_hTc, n + CR)
                        for c, (at, size) in enumerate(FCH):
                            last = nc.tensor.transpose(FHT[0:size, c * P:(c + 1) * P], hm[:, i % 2, at:at + size], ident[:])
                        last.then_inc(f_hT, 1)
                        if i + 2 < FT:
                            hidden(i + 2)
                        pe.wait_ge(f_hTc, n + (1 + CR))
                        if i == 0:
                            pe.wait_ge(x_full, L * B + f * 2 + B)
                        for c, (at, size) in enumerate(FCH):
                            last = mm(FZ[:, i * D:(i + 1) * D], hT[0:size, i % 2, c * P:(c + 1) * P], w2[0:size, c, :],
                                      start=(c == 0), stop=(c == 2))
                    last.then_inc(f_z, 1)


def _constants():
    f32 = np.float32
    ident = np.eye(P, dtype=f32)
    q = np.arange(P)[:, None]
    even = np.arange(P)[None, :]
    odd = np.arange(WIDE)[None, :] - WIN
    band = lambda k: np.where((k > q) | (k < q - WIN), f32(MASKED), f32(0))
    masks = np.concatenate([band(even), band(odd), np.where(even > q, f32(MASKED), f32(0))], 1).astype(f32)
    center = (ident - f32(1.0 / D)).astype(f32)
    half = np.arange(0, DH, 2, dtype=f32)
    inv_freq = f32(1.0) / np.power(f32(10000.0), half / f32(DH), dtype=f32)
    t = np.arange(S, dtype=f32)
    freqs = t[:, None] * inv_freq[None, :]
    freqs = np.concatenate([freqs, freqs], -1)
    base = (half + f32(0.4 * DH)) / f32(1.4 * DH)
    power = (t - f32(S // 2)) / f32(WIN // 2)
    scale = np.power(base[None, :], power[:, None], dtype=f32)
    scale = np.concatenate([scale, scale], -1)
    sign = np.where(np.arange(DH) < DH // 2, f32(-1), f32(1))
    cos, sin = np.cos(freqs).astype(f32), np.sin(freqs).astype(f32) * sign
    inv = f32(1.0) / scale
    rope = np.stack([cos * inv, sin * inv, cos * scale * f32(QK_SCALE), sin * scale * f32(QK_SCALE)], 0)
    rope = rope.reshape(4, TPB, P, DH).transpose(2, 0, 1, 3)
    return {"ident": ident, "masks": masks, "center": center, "rope": np.ascontiguousarray(rope.astype(f32))}


_INS = ['L0_attn_x', 'L0_attn_Wq', 'L0_attn_Wk', 'L0_attn_Wv', 'L0_attn_Wo', 'L0_ffn_Wqkv', 'L0_ffn_q_scale',
        'L0_ffn_k_scale', 'L0_ffn_Wo', 'L0_ffn_ln_g', 'L0_ffn_ln_b', 'L0_ffn_W1', 'L0_ffn_b1', 'L0_ffn_W2',
        'L0_ffn_b2', 'L0_c', 'L0_wmod']


def kernel(**inputs):
    import concourse.bacc as bacc
    from concourse.bass_utils import run_bass_kernel_spmd as run

    nc = bacc.Bacc("TRN2", target_bir_lowering=False, num_devices=1)
    arrays, args = {}, []
    named = [(n, np.ascontiguousarray(inputs[n])) for n in _INS] + list(_constants().items())
    for name, a in named:
        arrays[f"in_{name}"] = a
        args.append(nc.dram_tensor(f"in_{name}", a.shape, mybir.dt.from_np(a.dtype), kind="ExternalInput").ap())
    args.append(nc.dram_tensor("out_0", (B, S, D), F32, kind="ExternalOutput").ap())
    build(nc, *args)
    r = run(nc, [arrays], core_ids=[0])
    return r.results[0]["out_0"]
```

```python
from contextlib import ExitStack

import numpy as np
import concourse.bass as bass
from concourse import mybir

F32 = mybir.dt.float32
BF16 = mybir.dt.bfloat16
ACT = mybir.ActivationFunctionType
ALU = mybir.AluOpType
AX = mybir.AxisListType

P = 128
D = 128
B, S = 16, 256
TPB = S // P
NT = B * TPB
DEPTH = 6
H, DH = 16, 64
INNER = H * DH
PAIRS = H // 2
WIN = 32
WIDE = WIN + P
F = 341
FCH = [(0, 128), (128, 128), (256, 85)]
HPC = 8
CH = HPC * DH
KQ = 4
AT = NT + 1
YT = NT + 2
FT = 4
NF = NT // FT
MASKED = -3.0e38
EPS = 1e-5
RMS_SCALE = float(D) ** -0.5
POOL_SETUP = 9
QK_SCALE = 8.0
ATT1_SCALE = float(D) ** -0.5
CR = 2
CHUNK_COL = [INNER, 0, INNER + CH, CH, 2 * INNER, 2 * INNER + CH]


def build(nc, a_x, a_wq, a_wk, a_wv, a_wo, f_wqkv, f_qs, f_ks, f_wo, f_g, f_b, f_w1, f_b1, f_w2, f_b2,
          c_in, wmod, ident_in, masks_in, center_in, rope_in, out):
    with ExitStack() as ctx:
        def sb(name, shape, dt=F32):
            return ctx.enter_context(nc.sbuf_tensor(name, shape, dt))

        def sem(name):
            return ctx.enter_context(nc.semaphore(name))

        bank = [ctx.enter_context(nc.psum_tensor(f"bank{i}", [P, 512], F32)) for i in range(8)]

        ident = sb("ident", [P, P])
        identb = sb("identb", [P, P], BF16)
        mask_f = sb("mask_f", [P, P + WIDE + P])
        masks = sb("masks", [P, P + WIDE + P], BF16)
        mask_even, mask_odd, mask_causal = masks[:, 0:P], masks[:, P:P + WIDE], masks[:, P + WIDE:]
        center = sb("center", [P, P])
        rope = sb("rope", [P, 4, TPB, DH])
        neg_half = sb("neg_half", [P, HPC])
        eps = sb("eps", [P, HPC])
        x = sb("x", [P, 1 + NT + FT, D])
        x1 = sb("x1", [P, NT, D])
        gb = sb("gb", [P, B, D])
        w1q, w1k, w1v, w1o = (sb(f"w1{n}", [P, D]) for n in "qkvo")
        wmod_s = sb("wmod_s", [P, 6 * D])
        crow = sb("crow", [B, D])
        cT = sb("cT", [P, B])
        csig = sb("csig", [P, B])
        cden = sb("cden", [P, B])
        cinv = sb("cinv", [P, B])
        csilu = sb("csilu", [P, B])
        cb_l = sb("cb_l", [P, P])
        mod = sb("mod", [P, 6, D])
        gate_sign = sb("gate_sign", [P, 2, D])
        gate_pos = sb("gate_pos", [P, 2, D])
        gate_abs = sb("gate_abs", [P, 2, D])
        tsum = sb("tsum", [P, TPB])
        nmean = sb("nmean", [P, TPB])
        xc = sb("xc", [P, TPB, D])
        sqj = sb("sqj", [P, TPB, D])
        ssq = sb("ssq", [P, TPB])
        var1 = sb("var1", [P, TPB])
        rstd = sb("rstd", [P, TPB])
        h1 = sb("h1", [P, TPB, D])
        h1s = sb("h1s", [P, TPB, D])
        ga = sb("ga", [P, D])
        xn = sb("xn", [P, TPB, D])
        h1T = sb("h1T", [P, S])
        q1T = sb("q1T", [P, S])
        k1T = sb("k1T", [P, S])
        v1 = sb("v1", [P, TPB, D])
        nm1 = sb("nm1", [P, TPB])
        nms1 = sb("nms1", [P, TPB])
        sum1 = sb("sum1", [P, TPB])
        rin1 = sb("rin1", [P, TPB])
        p1 = sb("p1", [P, P + S])
        p1T = sb("p1T", [P, 3 * P])
        o1T = sb("o1T", [P, S])
        att1 = sb("att1", [P, TPB, D])
        wqkv = sb("wqkv", [P, 3 * INNER])
        wo = sb("wo", [P, PAIRS, D])
        scales = sb("scales", [P, 2, DH])
        tables = sb("tables", [P, 4, TPB, DH])
        w1 = sb("w1", [P, 2 * F])
        w1g = sb("w1g", [P, 2 * F])
        w1c = sb("w1c", [P, 2 * F])
        w2 = sb("w2", [P, 3, D])
        lng = sb("lng", [P, 1])
        lnb = sb("lnb", [P, 1])
        lnb_l = sb("lnb_l", [P, P])
        b1r = sb("b1r", [P, 2 * F])
        b2r = sb("b2r", [P, D])
        bias1 = sb("bias1", [P, 2 * F])
        xs = sb("xs", [P, D])
        yT = sb("yT", [P, S + 1])
        sq = sb("sq", [P, 2, CH])
        rc = sb("rc", [P, 2, CH])
        rs = sb("rs", [P, 2, CH])
        rsum = sb("rsum", [P, 2, CH])
        rot = sb("rot", [P, 2, CH])
        n2 = sb("n2", [P, KQ, HPC])
        n2g = sb("n2g", [P, KQ, HPC])
        rn = sb("rn", [P, KQ, HPC])
        qT = sb("qT", [P, 2, 2, PAIRS, P])
        kTe = sb("kTe", [P, PAIRS, P])
        kTo = sb("kTo", [P, PAIRS, WIDE])
        v = sb("v", [P, 2, INNER])
        vt = sb("vt", [WIN, INNER])
        nmax = sb("nmax", [P, 2, 2])
        psm = sb("psm", [P, 2, 2])
        pinv = sb("pinv", [P, 2, 2])
        pr = sb("pr", [P, 2, 2, WIDE])
        pT = sb("pT", [P, 2, 2 * P + 2 * WIN])
        oT = sb("oT", [P, PAIRS, P])
        xsf = sb("xsf", [P, FT, D])
        xbf = sb("xbf", [P, 2, FT, D])
        yTf = sb("yTf", [P, 2, FT // TPB, S + 1])
        sqf = sb("sqf", [P, FT, D])
        ssf = sb("ssf", [P, FT])
        vaf = sb("vaf", [P, FT])
        rsf = sb("rsf", [P, 2, FT])
        ha = sb("ha", [P, 2, F])
        hg = sb("hg", [P, 2, F])
        gg = sb("gg", [P, 2, F])
        hm = sb("hm", [P, 2, F])
        hT = sb("hT", [P, 2, 3 * P])

        const_in, out_done, attn_w_in, ffn_w_in = (sem(n) for n in ("const_in", "out_done", "attn_w_in", "ffn_w_in"))
        pool_setup, dve_setup, pe_setup, act_setup = (sem(n) for n in ("pool_setup", "dve_setup", "pe_setup", "act_setup"))
        m_act, m_dve, m_pe, m_pool = (sem(n) for n in ("m_act", "m_dve", "m_pe", "m_pool"))
        x_full = sem("x_full")
        tables_done = sem("tables_done")
        xs_ready, xT_done, yT_ready = (sem(n) for n in ("xs_ready", "xT_done", "yT_ready"))
        chunk_done, sq_done, prod_done, red_done = (sem(n) for n in ("chunk_done", "sq_done", "prod_done", "red_done"))
        rsum_done, guard_done, rn_done, rot_done = (sem(n) for n in ("rsum_done", "guard_done", "rn_done", "rot_done"))
        rot_turned, t_copied, v_done = (sem(n) for n in ("rot_turned", "t_copied", "v_done"))
        ktail_done, vtail_done = sem("ktail_done"), sem("vtail_done")
        sims_done, max_done, exp_done, inv_done, norm_done = (
            sem(n) for n in ("sims_done", "max_done", "exp_done", "inv_done", "norm_done"))
        pt_done, pt_copied, pv_done, o_copied, wo_done, x_upd = (
            sem(n) for n in ("pt_done", "pt_copied", "pv_done", "o_copied", "wo_done", "x_upd"))
        w1g_done, w1c_mm, w1c_done, bias_mm, bias_done = (
            sem(n) for n in ("w1g_done", "w1c_mm", "w1c_done", "bias_mm", "bias_done"))
        f_xs, f_xT, f_yT, f_yc, f_ss, f_var, f_rstd = (
            sem(n) for n in ("f_xs", "f_xT", "f_yT", "f_yc", "f_ss", "f_var", "f_rstd"))
        f_h, f_hb, f_gelu, f_hm, f_hT, f_hTc, f_z = (
            sem(n) for n in ("f_h", "f_hb", "f_gelu", "f_hm", "f_hT", "f_hTc", "f_z"))
        scaled, gated = sem("scaled"), sem("gated")

        G = [bank[0], bank[1]]
        T = bank[2]
        SIM = [bank[3], bank[4]]
        PT = bank[5]
        O = bank[6]
        Z = bank[7]
        FH = [(bank[5], bank[6]), (bank[0], bank[1])]
        FT_B, FYC, FHT, FZ = bank[2], bank[3], bank[4], bank[7]

        N_CONST, N_ATTN, N_FFN = 12, 4, 7
        DA, AA, PA, GA = 26, 12, 7, 4

        def settle(eng):
            eng.wait_ge(pool_setup, POOL_SETUP)

        block = ctx.enter_context(nc.Block())

        @block.sync
        def _(sp):
            x_dram = a_x.rearrange("b (t p) d -> p (b t) d", p=P)
            o_dram = out.rearrange("b (t p) d -> p (b t) d", p=P)
            for dst, src in ((crow[:], c_in), (ident[:], ident_in), (wmod_s[:], wmod), (mask_f[:], masks_in),
                             (w1q[:], a_wq), (w1k[:], a_wk), (w1v[:], a_wv), (w1o[:], a_wo),
                             (center[:], center_in), (rope[:], rope_in)):
                sp.dma_start(dst, src).then_inc(const_in, 16)
            for i in range(2):
                half = slice(i * NT // 2, (i + 1) * NT // 2)
                sp.dma_start(x1[:, half, :], x_dram[:, half, :]).then_inc(const_in, 16)
            with sp.Fori(0, DEPTH) as L:
                sp.wait_ge(v_done, L * (2 * AT) + CR)
                sp.wait_ge(prod_done, L * (KQ * AT) + CR)
                sp.wait_ge(x_upd, L * (NT + 1) + CR)
                sp.dma_start(wqkv[:], f_wqkv[bass.ds(L, 1)].rearrange("l p n -> p (l n)")).then_inc(attn_w_in, 16)
                sp.dma_start(wo[:], f_wo[bass.ds(L, 1)].rearrange("l (c p) n -> p (l c) n", p=P)).then_inc(attn_w_in, 16)
                sp.dma_start(scales[:, 0, :], f_ks[bass.ds(L, 1)].to_broadcast([P, DH])).then_inc(attn_w_in, 16)
                sp.dma_start(scales[:, 1, :], f_qs[bass.ds(L, 1)].to_broadcast([P, DH])).then_inc(attn_w_in, 16)
                sp.wait_ge(x_full, (L + 1) * B)
                sp.dma_start(w1[:], f_w1[bass.ds(L, 1)].rearrange("l p n -> p (l n)")).then_inc(ffn_w_in, 16)
                sp.dma_start(w2[:, 0:2, :], f_w2[bass.ds(L, 1), 0:2 * P].rearrange("l (c p) n -> p (l c) n", p=P)).then_inc(ffn_w_in, 16)
                sp.dma_start(w2[0:F - 2 * P, 2, :], f_w2[bass.ds(L, 1), 2 * P:F].rearrange("l p n -> p (l n)")).then_inc(ffn_w_in, 16)
                sp.dma_start(lng[:], f_g[bass.ds(L, 1)].rearrange("l p -> p l")).then_inc(ffn_w_in, 16)
                sp.dma_start(lnb[:], f_b[bass.ds(L, 1)].rearrange("l p -> p l")).then_inc(ffn_w_in, 16)
                sp.dma_start(b1r[:], f_b1[bass.ds(L, 1)].to_broadcast([P, 2 * F])).then_inc(ffn_w_in, 16)
                sp.dma_start(b2r[:], f_b2[bass.ds(L, 1)].to_broadcast([P, D])).then_inc(ffn_w_in, 16)
                with sp.Fori(0, B) as j:
                    sp.wait_ge(v_done, (L * AT + j * 2) * 2 + (2 + CR))
                    sp.wait_ge(pv_done, (L * NT + j * 2) * PAIRS + CR)
                    sp.dma_start(vt[:], v[P - WIN:P, 0, :]).then_inc(vtail_done, 16)
            for i in range(4):
                part = slice(i * NT // 4, (i + 1) * NT // 4)
                sp.wait_ge(gated, i + 1)
                sp.dma_start(o_dram[:, part, :], x[:, 1 + i * NT // 4:1 + (i + 1) * NT // 4, :]).then_inc(out_done, 16)
            sp.wait_ge(out_done, 64)

        @block.gpsimd
        def _(pool):
            for s in (xs_ready, rsum_done, guard_done, rn_done, rot_done, f_var, f_rstd, f_hm):
                pool.sem_inc(s, CR)
            nc.gpsimd.memset(neg_half[:], -0.5).then_inc(pool_setup, 1)
            nc.gpsimd.memset(eps[:], EPS).then_inc(pool_setup, 1)
            nc.gpsimd.memset(x[:, 0, :], 0.0).then_inc(pool_setup, 1)
            nc.gpsimd.memset(x[:, NT + 1:, :], 0.0).then_inc(pool_setup, 1)
            nc.gpsimd.memset(oT[:], 0.0).then_inc(pool_setup, 1)
            nc.gpsimd.memset(yTf[:, :, :, 0:1], 0.0).then_inc(pool_setup, 1)
            nc.gpsimd.memset(yT[:, 0:1], 0.0).then_inc(pool_setup, 1)
            pool.wait_ge(pool_setup, POOL_SETUP - 2)
            nc.gpsimd.memset(qT[0:DH, :, 1], 0.0).then_inc(pool_setup, 1)
            pool.wait_ge(pool_setup, POOL_SETUP - 1)
            nc.gpsimd.memset(qT[DH:P, :, 0], 0.0).then_inc(pool_setup, 1)
            pool.wait_ge(pool_setup, POOL_SETUP)

            with pool.Fori(0, B) as b:
                for half in range(2):
                    pool.wait_ge(m_act, b * AA + (3, AA)[half])
                    nc.gpsimd.tensor_tensor(var1[:], ssq[:], eps[:, 0:TPB], ALU.add).then_inc(m_pool, 1)
                    pool.wait_ge(m_pool, b * GA + (2 * half + 1))
                    nc.gpsimd.tensor_tensor(rstd[:], var1[:], neg_half[:, 0:TPB], ALU.pow).then_inc(m_pool, 1)

            def load_x(tile):
                nc.gpsimd.tensor_copy(xs[:], x[:, tile, :].rearrange("p a d -> p (a d)")).then_inc(xs_ready, 1)

            def rotate(a, following):
                for c in range(KQ):
                    n = a * KQ + c
                    slot = c % 2
                    pool.wait_ge(prod_done, n + (1 + CR))
                    nc.gpsimd.tensor_tensor(rsum[:, slot, :], rc[:, slot, :], rs[:, slot, :], ALU.add).then_inc(rsum_done, 1)
                    if c == 0:
                        load_x(following)
                    settle(pool)
                    pool.wait_ge(red_done, n + (1 + CR))
                    nc.gpsimd.tensor_scalar(n2g[:, c, :], n2[:, c, :], 1e-24, None, ALU.max).then_inc(guard_done, 1)
                    pool.wait_ge(guard_done, n + (1 + CR))
                    nc.gpsimd.tensor_tensor(rn[:, c, :], n2g[:, c, :], neg_half[:], ALU.pow).then_inc(rn_done, 1)
                    pool.wait_ge(rn_done, n + (1 + CR))
                    pool.wait_ge(rot_turned, n + (CR - 1))
                    nc.gpsimd.tensor_tensor(
                        rot[:, slot, :].rearrange("p (h d) -> p h d", d=DH),
                        rsum[:, slot, :].rearrange("p (h d) -> p h d", d=DH),
                        rn[:, c, :, None].to_broadcast([P, HPC, DH]), ALU.mult).then_inc(rot_done, 1)

            with pool.Fori(0, DEPTH) as L:
                pool.wait_ge(attn_w_in, (L + 1) * (16 * N_ATTN))
                pool.wait_ge(x_full, (L + 1) * B)
                for i in range(4):
                    s = scales[:, i // 2, :].rearrange("p (x d) -> p x d", x=2)
                    if i % 2:
                        s = s[:, ::-1, :]
                    for t in range(TPB):
                        nc.gpsimd.tensor_tensor(
                            tables[:, i, t, :].rearrange("p (x d) -> p x d", x=2),
                            rope[:, i, t, :].rearrange("p (x d) -> p x d", x=2), s, ALU.mult).then_inc(tables_done, 1)
                load_x(bass.ds(1, 1))
                rotate(L * AT, bass.ds(2, 1))
                with pool.Fori(0, B) as j:
                    for par in range(2):
                        rotate(L * AT + j * 2 + par + 1, bass.ds(j * 2 + par + 3, 1))
                def rstd_ffn(k, slot):
                    pool.wait_ge(f_ss, k * FT + (FT + CR))
                    nc.gpsimd.tensor_tensor(vaf[:], ssf[:], eps[:, 0:FT], ALU.add).then_inc(f_var, 1)
                    pool.wait_ge(f_var, k + (1 + CR))
                    nc.gpsimd.tensor_tensor(rsf[:, slot, :], vaf[:], neg_half[:, 0:FT], ALU.pow).then_inc(f_rstd, 1)

                rstd_ffn(L * (NF + 1), 0)
                with pool.Fori(0, NF // 2) as f:
                    for slot in range(2):
                        k = L * (NF + 1) + f * 2 + slot
                        m = (L * NF + f * 2 + slot) * FT
                        for i in range(FT):
                            pool.wait_ge(f_gelu, m + (i + 1 + CR))
                            pool.wait_ge(f_hT, m + (i - 1 + CR))
                            nc.gpsimd.tensor_tensor(hm[:, i % 2, :], ha[:, i % 2, :], gg[:, i % 2, :], ALU.mult).then_inc(f_hm, 1)
                            if i == 1:
                                rstd_ffn(k + 1, 1 - slot)

        @block.scalar
        def _(act):
            for s in (yT_ready, sq_done, t_copied, ktail_done, v_done, exp_done, pt_copied, o_copied,
                      w1c_done, f_yT, f_ss, f_gelu, f_hTc):
                act.sem_inc(s, CR)
            act.wait_ge(dve_setup, 11)
            nc.scalar.activation(csig[:], cT[:], ACT.Exp, scale=-1.0).then_inc(act_setup, 1)

            with act.Fori(0, B) as b:
                act.wait_ge(m_pe, b * PA + 1)
                nc.scalar.activation(mod[:, 0:3, :], bank[0][:, 0:3 * D].rearrange("p (a d) -> p a d", d=D), ACT.Copy)
                nc.scalar.activation(mod[:, 3:6, :], bank[1][:, 0:3 * D].rearrange("p (a d) -> p a d", d=D), ACT.Copy).then_inc(m_act, 1)
                act.wait_ge(m_dve, b * DA + 4)
                nc.scalar.activation(sqj[:, 0, :], xc[:, 0, :], ACT.Square, scale=RMS_SCALE, accum_out=ssq[:, 0:1]).then_inc(m_act, 1)
                nc.scalar.activation(sqj[:, 1, :], xc[:, 1, :], ACT.Square, scale=RMS_SCALE, accum_out=ssq[:, 1:2]).then_inc(m_act, 1)
                act.wait_ge(m_pe, b * PA + 2)
                nc.scalar.activation(h1T[:], bank[2][:, 0:S], ACT.Copy).then_inc(m_act, 1)
                act.wait_ge(m_pe, b * PA + 3)
                nc.scalar.activation(q1T[:], bank[3][:, 0:S], ACT.Copy).then_inc(m_act, 1)
                nc.scalar.activation(k1T[:], bank[4][:, 0:S], ACT.Copy).then_inc(m_act, 1)
                act.wait_ge(m_dve, b * DA + 16)
                nc.scalar.activation(p1[:, 0:P], bank[6][:, 0:P], ACT.Exp, scale=ATT1_SCALE, bias=nms1[:, 0:1],
                                     accum_out=sum1[:, 0:1]).then_inc(m_act, 1)
                nc.scalar.activation(p1[:, P:P + S], bank[6][:, P:P + S], ACT.Exp, scale=ATT1_SCALE, bias=nms1[:, 1:2],
                                     accum_out=sum1[:, 1:2]).then_inc(m_act, 1)
                act.wait_ge(m_pe, b * PA + 5)
                nc.scalar.activation(p1T[:], bank[7][:, 0:3 * P], ACT.Copy).then_inc(m_act, 1)
                act.wait_ge(m_pe, b * PA + 6)
                nc.scalar.activation(o1T[:], bank[0][:, 0:S], ACT.Copy).then_inc(m_act, 1)
                act.wait_ge(m_dve, b * DA + 24)
                nc.scalar.activation(sqj[:, 0, :], xc[:, 0, :], ACT.Square, scale=RMS_SCALE, accum_out=ssq[:, 0:1]).then_inc(m_act, 1)
                nc.scalar.activation(sqj[:, 1, :], xc[:, 1, :], ACT.Square, scale=RMS_SCALE, accum_out=ssq[:, 1:2]).then_inc(m_act, 1)

            def exps(g, s, N):
                act.wait_ge(max_done, g + (s + 1 + CR))
                act.wait_ge(pt_done, g + (s - 1 + CR))
                slot = s % 2
                for h in range(2):
                    last = nc.scalar.activation(pr[:, slot, h, 0:N], SIM[slot][:, h * N:(h + 1) * N], ACT.Exp,
                                                bias=nmax[:, slot, h:h + 1], accum_out=psm[:, slot, h:h + 1])
                last.then_inc(exp_done, 1)

            def pt_copy(g, s, par):
                act.wait_ge(pt_done, g + (s + 1 + CR))
                act.wait_ge(pv_done, g + (s - 1 + CR))
                n = 2 * P + (2 * WIN if par else 0)
                nc.scalar.activation(pT[:, s % 2, 0:n], PT[:, 0:n], ACT.Copy).then_inc(pt_copied, 1)

            def o_copy(b, w, half):
                act.wait_ge(pv_done, b * PAIRS + (4 * half + 4 + CR))
                act.wait_ge(wo_done, w + (1 + CR))
                nc.scalar.activation(oT[:, 4 * half:4 * half + 4, :], O[:].rearrange("p (c t) -> p c t", c=4),
                                     ACT.Copy).then_inc(o_copied, 1)

            def y_copy(y, par):
                act.wait_ge(xT_done, y + (1 + CR))
                nc.scalar.activation(yT[0:64, par * P:(par + 1) * P], T[0:64, 0:P], ACT.Copy)
                nc.scalar.activation(yT[64:P, par * P + 1:(par + 1) * P + 1], T[64:P, 0:P], ACT.Copy).then_inc(yT_ready, 1)

            def square(a, c):
                act.wait_ge(chunk_done, a * 6 + (c + 1 + CR))
                act.wait_ge(red_done, a * KQ + (c - 1 + CR))
                nc.scalar.activation(sq[:, c % 2, :], G[c % 2][:], ACT.Square).then_inc(sq_done, 1)

            def t_copy(a, c, par):
                act.wait_ge(rot_turned, a * KQ + (c + 1 + CR))
                half = slice(4 * (c // 2), 4 * (c // 2) + 4)
                src = T[:].rearrange("p (c t) -> p c t", c=4)
                if c % 2:
                    nc.scalar.activation(qT[0:DH, par, 0, half, :], src[0:DH], ACT.Copy)
                    nc.scalar.activation(qT[DH:P, par, 1, half, :], src[DH:P], ACT.Copy).then_inc(t_copied, 1)
                    return
                if par:
                    dst = kTo[:, half, WIN:WIDE]
                else:
                    dst = kTe[:, half, :]
                nc.scalar.activation(dst, src, ACT.Copy).then_inc(t_copied, 1)

            def v_copy(a, c, par):
                act.wait_ge(chunk_done, a * 6 + (KQ + c + 1 + CR))
                nc.scalar.activation(v[:, par, c * CH:(c + 1) * CH], G[c % 2][:], ACT.Copy).then_inc(v_done, 1)

            def tile(b, a, y, w, par, batch):
                g = b * PAIRS
                N = WIDE if par else P
                nxt = 1 - par
                exps(g, 0, N)
                for s in range(PAIRS):
                    if s + 1 < PAIRS:
                        exps(g, s + 1, N)
                    pt_copy(g, s, par)
                    if s < 2:
                        t_copy(a - 1, s + 2, par)
                    if s == 3 and nxt:
                        act.wait_ge(sims_done, g + (5 + CR))
                        nc.scalar.activation(kTo[:, :, 0:WIN], kTe[:, :, P - WIN:P], ACT.Copy).then_inc(ktail_done, 1)
                    if s < KQ:
                        square(a, s)
                    if s == 4:
                        t_copy(a, 0, nxt)
                    if s == 5:
                        o_copy(b, w, 0)
                        if not nxt:
                            act.wait_ge(vtail_done, batch * 16 + 16)
                        v_copy(a, 0, nxt)
                    if s == 6:
                        t_copy(a, 1, nxt)
                v_copy(a, 1, nxt)
                y_copy(y + 1, par)
                o_copy(b, w, 1)

            with act.Fori(0, DEPTH) as L:
                y_copy(L * YT, 0)
                for c in range(KQ):
                    square(L * AT, c)
                for c in range(2):
                    t_copy(L * AT, c, 0)
                for c in range(2):
                    v_copy(L * AT, c, 0)
                y_copy(L * YT + 1, 1)
                with act.Fori(0, B) as j:
                    for par in range(2):
                        t = j * 2 + par
                        tile(L * NT + t, L * AT + t + 1, L * YT + t + 1, L * (NT + 1) + t, par, L * B + j)
                for c in range(2, KQ):
                    t_copy(L * AT + NT, c, 0)
                act.wait_ge(w1c_mm, L + (1 + CR))
                nc.scalar.activation(w1c[:, 0:F], bank[0][:, 0:F], ACT.Copy)
                nc.scalar.activation(w1c[:, F:2 * F], bank[1][:, 0:F], ACT.Copy).then_inc(w1c_done, 1)
                def front(k, slot):
                    act.wait_ge(f_xT, k + (1 + CR))
                    turned = FT_B[:].rearrange("p (b t) -> p b t", b=FT // TPB)
                    nc.scalar.activation(yTf[0:64, slot, :, 0:S], turned[0:64], ACT.Copy)
                    nc.scalar.activation(yTf[64:P, slot, :, 1:S + 1], turned[64:P], ACT.Copy).then_inc(f_yT, 1)

                def squares(k):
                    act.wait_ge(f_yc, k + (1 + CR))
                    for i in range(FT):
                        nc.scalar.activation(sqf[:, i, :], FYC[:, i * P:(i + 1) * P], ACT.Square, scale=RMS_SCALE,
                                             accum_out=ssf[:, i:i + 1]).then_inc(f_ss, 1)

                front(L * (NF + 1), 0)
                squares(L * (NF + 1))
                with act.Fori(0, NF // 2) as f:
                    for slot in range(2):
                        k = L * (NF + 1) + f * 2 + slot
                        m = (L * NF + f * 2 + slot) * FT
                        for i in range(FT + 1):
                            if i < FT:
                                act.wait_ge(f_hb, m + (i + 1 + CR))
                                act.wait_ge(f_hm, m + (i - 1 + CR))
                                nc.scalar.activation(gg[:, i % 2, :], hg[:, i % 2, :], ACT.Gelu).then_inc(f_gelu, 1)
                            if i >= 1:
                                act.wait_ge(f_hT, m + (i + CR))
                                nc.scalar.activation(hT[:, (i - 1) % 2, :], FHT[:, 0:3 * P], ACT.Copy).then_inc(f_hTc, 1)
                            if i == 0:
                                front(k + 1, 1 - slot)
                            if i == 1:
                                squares(k + 1)

        @block.vector
        def _(dve):
            for s in (red_done, prod_done, max_done, inv_done, norm_done, x_upd, w1g_done, bias_done, f_xs, f_hb):
                dve.sem_inc(s, CR)
            for i in range(8):
                nc.vector.memset(bank[i][:], 0.0).then_inc(dve_setup, 1)
            dve.wait_ge(const_in, 16 * N_CONST)
            nc.vector.tensor_copy(identb[:], ident[:]).then_inc(dve_setup, 1)
            nc.vector.tensor_copy(masks[:], mask_f[:]).then_inc(dve_setup, 1)
            dve.wait_ge(pe_setup, 1)
            nc.vector.tensor_copy(cT[:], bank[0][:, 0:B]).then_inc(dve_setup, 1)
            dve.wait_ge(act_setup, 1)
            nc.vector.tensor_scalar(cden[:], csig[:], 1.0, None, ALU.add).then_inc(dve_setup, 1)
            dve.wait_ge(dve_setup, 12)
            nc.vector.reciprocal(cinv[:], cden[:]).then_inc(dve_setup, 1)
            dve.wait_ge(dve_setup, 13)
            nc.vector.tensor_tensor(csilu[:], cT[:], cinv[:], ALU.mult).then_inc(dve_setup, 1)
            dve.wait_ge(dve_setup, 14)

            with dve.Fori(0, B) as b:
                tiles = bass.ds(b * TPB, TPB)
                stream = bass.ds(b * TPB + 1, TPB)
                at = b * DA

                def centred(first, src):
                    nc.vector.tensor_reduce(tsum[:], src, AX.X, ALU.add).then_inc(m_dve, 1)
                    dve.wait_ge(m_dve, at + first)
                    nc.vector.tensor_scalar(nmean[:], tsum[:], -1.0 / D, None, ALU.mult).then_inc(m_dve, 1)
                    dve.wait_ge(m_dve, at + (first + 1))
                    nc.vector.tensor_tensor(xc[:], src, nmean[:, :, None].to_broadcast([P, TPB, D]),
                                            ALU.add).then_inc(m_dve, 1)

                nc.vector.tensor_copy(cb_l[:], csilu[:, bass.ds(b, 1)].to_broadcast([P, P])).then_inc(m_dve, 1)
                centred(2, x1[:, tiles, :])
                dve.wait_ge(m_act, b * AA + 1)
                nc.vector.tensor_scalar(mod[:, 1::3, :], mod[:, 1::3, :], 1.0, None, ALU.add)
                nc.vector.tensor_scalar(gate_pos[:], mod[:, 2::3, :], 0.25, None, ALU.max).then_inc(m_dve, 1)
                nc.vector.tensor_scalar(gate_sign[:], mod[:, 2::3, :], 0.0, 2.0, ALU.is_ge, ALU.mult).then_inc(m_dve, 1)
                dve.wait_ge(m_dve, at + 5)
                nc.vector.scalar_tensor_tensor(out=gate_abs[:], in0=mod[:, 2::3, :], scalar=-1.0, in1=gate_pos[:],
                                               op0=ALU.mult, op1=ALU.max).then_inc(m_dve, 1)
                dve.wait_ge(m_dve, at + 7)
                nc.vector.scalar_tensor_tensor(out=ga[:], in0=gate_sign[:, 0, :], scalar=-1.0, in1=gate_abs[:, 0, :],
                                               op0=ALU.add, op1=ALU.mult).then_inc(m_dve, 1)
                nc.vector.scalar_tensor_tensor(out=gb[:, bass.ds(b, 1), :].rearrange("p a d -> p (a d)"), in0=gate_sign[:, 1, :],
                                               scalar=-1.0, in1=gate_abs[:, 1, :], op0=ALU.add, op1=ALU.mult).then_inc(m_dve, 1)
                dve.wait_ge(m_pool, b * GA + 2)
                for t in range(TPB):
                    nc.vector.scalar_tensor_tensor(out=h1[:, t, :], in0=xc[:, t, :], scalar=rstd[:, t:t + 1], in1=mod[:, 1, :],
                                                   op0=ALU.mult, op1=ALU.mult).then_inc(m_dve, 1)
                dve.wait_ge(m_dve, at + 11)
                nc.vector.tensor_tensor(h1s[:], h1[:], mod[:, 0:1, :].to_broadcast([P, TPB, D]), ALU.add).then_inc(m_dve, 1)
                dve.wait_ge(m_pe, b * PA + 3)
                nc.vector.tensor_copy(v1[:], bank[5][:, 0:S].rearrange("p (t d) -> p t d", t=TPB)).then_inc(m_dve, 1)
                dve.wait_ge(m_pe, b * PA + 4)
                nc.vector.tensor_reduce(nm1[:, 0:1], bank[6][:, 0:P], AX.X, ALU.max, negate=True).then_inc(m_dve, 1)
                nc.vector.tensor_reduce(nm1[:, 1:2], bank[6][:, P:P + S], AX.X, ALU.max, negate=True).then_inc(m_dve, 1)
                dve.wait_ge(m_dve, at + 15)
                nc.vector.tensor_scalar(nms1[:], nm1[:], ATT1_SCALE, None, ALU.mult).then_inc(m_dve, 1)
                dve.wait_ge(m_act, b * AA + 8)
                nc.vector.reciprocal(rin1[:], sum1[:]).then_inc(m_dve, 1)
                dve.wait_ge(m_dve, at + 17)
                nc.vector.tensor_scalar(p1[:, 0:P], p1[:, 0:P], rin1[:, 0:1], None, ALU.mult).then_inc(m_dve, 1)
                nc.vector.tensor_scalar(p1[:, P:P + S], p1[:, P:P + S], rin1[:, 1:2], None, ALU.mult).then_inc(m_dve, 1)
                dve.wait_ge(m_pe, b * PA + 7)
                nc.vector.tensor_tensor(att1[:], bank[1][:, 0:S].rearrange("p (t d) -> p t d", t=TPB),
                                        ga[:, None, :].to_broadcast([P, TPB, D]), ALU.mult).then_inc(m_dve, 1)
                dve.wait_ge(m_dve, at + 20)
                nc.vector.tensor_tensor(xn[:], x1[:, tiles, :], att1[:], ALU.add).then_inc(m_dve, 1)
                dve.wait_ge(m_dve, at + 21)
                centred(22, xn[:])
                nc.vector.tensor_copy(x1[:, tiles, :], xn[:])
                dve.wait_ge(m_pool, b * GA + 4)
                for t in range(TPB):
                    nc.vector.scalar_tensor_tensor(out=h1[:, t, :], in0=xc[:, t, :], scalar=rstd[:, t:t + 1], in1=mod[:, 4, :],
                                                   op0=ALU.mult, op1=ALU.mult).then_inc(m_dve, 1)
                dve.wait_ge(m_dve, at + 26)
                nc.vector.tensor_tensor(x[:, stream, :], h1[:], mod[:, 3:4, :].to_broadcast([P, TPB, D]), ALU.add).then_inc(x_full, 1)

            def products(a, c, par):
                dve.wait_ge(sq_done, a * KQ + (c + 1 + CR))
                dve.wait_ge(rsum_done, a * KQ + (c - 1 + CR))
                slot, which = c % 2, 2 * (c % 2)
                nc.vector.tensor_tensor(rc[:, slot, :].rearrange("p (h d) -> p h d", d=DH),
                                        G[slot][:].rearrange("p (h d) -> p h d", d=DH),
                                        tables[:, which, par:par + 1, :].to_broadcast([P, HPC, DH]), ALU.mult)
                nc.vector.tensor_tensor(
                    rs[:, slot, :].rearrange("p (h x d) -> p h x d", x=2, d=DH // 2),
                    G[slot][:].rearrange("p (h x d) -> p h x d", x=2, d=DH // 2)[:, :, ::-1, :],
                    tables[:, which + 1, par:par + 1, :].to_broadcast([P, HPC, DH]).rearrange("p h (x d) -> p h x d", x=2),
                    ALU.mult).then_inc(prod_done, 1)

            def norms(a, c):
                dve.wait_ge(sq_done, a * KQ + (c + 1 + CR))
                nc.vector.tensor_reduce(n2[:, c, :], sq[:, c % 2, :].rearrange("p (h d) -> p h d", d=DH), AX.X,
                                        ALU.add).then_inc(red_done, 1)

            def maxima(g, s, N):
                dve.wait_ge(sims_done, g + (s + 1 + CR))
                nc.vector.tensor_reduce(nmax[:, s % 2, :], SIM[s % 2][:, 0:2 * N].rearrange("p (h n) -> p h n", h=2), AX.X,
                                        ALU.max, negate=True).then_inc(max_done, 1)

            def normalise(g, s, N):
                slot = s % 2
                dve.wait_ge(exp_done, g + (s + 1 + CR))
                nc.vector.reciprocal(pinv[:, slot, :], psm[:, slot, :]).then_inc(inv_done, 1)
                dve.wait_ge(inv_done, g + (s + 1 + CR))
                for h in range(2):
                    last = nc.vector.tensor_scalar(pr[:, slot, h, 0:N], pr[:, slot, h, 0:N], pinv[:, slot, h:h + 1], None, ALU.mult)
                last.then_inc(norm_done, 1)

            def update(w, at):
                dve.wait_ge(wo_done, w + (1 + CR))
                xt = x[:, at, :].rearrange("p a d -> p (a d)")
                nc.vector.tensor_tensor(xt, Z[:, 0:D], xt, ALU.add).then_inc(x_upd, 1)

            def tile(b, a, w, par, at):
                g = b * PAIRS
                N = WIDE if par else P
                nxt = 1 - par
                maxima(g, 0, N)
                maxima(g, 1, N)
                for s in range(PAIRS):
                    normalise(g, s, N)
                    if s + 2 < PAIRS:
                        maxima(g, s + 2, N)
                    if s == 0:
                        update(w, at)
                    if 1 <= s <= KQ:
                        products(a, s - 1, nxt)
                        norms(a, s - 1)

            with dve.Fori(0, DEPTH) as L:
                dve.wait_ge(tables_done, L * 8 + 8)
                for c in range(KQ):
                    products(L * AT, c, 0)
                    norms(L * AT, c)
                with dve.Fori(0, B) as j:
                    for par in range(2):
                        t = j * 2 + par
                        tile(L * NT + t, L * AT + t + 1, L * (NT + 1) + t, par, bass.ds(t, 1))
                update(L * (NT + 1) + NT, bass.ds(NT, 1))
                dve.wait_ge(ffn_w_in, (L + 1) * (16 * N_FFN))
                nc.vector.tensor_scalar(w1g[:], w1[:], lng[:, 0:1], None, ALU.mult)
                nc.vector.tensor_copy(lnb_l[:], lnb[:, 0:1].to_broadcast([P, P])).then_inc(w1g_done, 1)
                dve.wait_ge(x_upd, (L + 1) * (NT + 1) + CR)
                dve.wait_ge(bias_mm, L + (1 + CR))
                nc.vector.tensor_tensor(bias1[:, 0:F], bank[5][:, 0:F], b1r[:, 0:F], ALU.add)
                nc.vector.tensor_tensor(bias1[:, F:2 * F], bank[6][:, 0:F], b1r[:, F:2 * F], ALU.add).then_inc(bias_done, 1)

                def front(k, slot, at):
                    nc.vector.tensor_tensor(xbf[:, slot], x[:, at, :], b2r[:, None, :].to_broadcast([P, FT, D]), ALU.add)
                    nc.vector.tensor_copy(xsf[:], x[:, at, :]).then_inc(f_xs, 1)

                front(L * (NF + 1), 0, bass.ds(1, FT))
                with dve.Fori(0, NF // 2) as f:
                    for slot in range(2):
                        k = L * (NF + 1) + f * 2 + slot
                        r = L * NF + f * 2 + slot
                        dve.wait_ge(f_xT, k + (1 + CR))
                        dve.wait_ge(x_full, (L + 1) * B + (f * 2 + slot) * 2)
                        front(k + 1, 1 - slot, bass.ds((f * 2 + slot + 1) * FT + 1, FT))
                        dve.wait_ge(f_rstd, k + (1 + CR))
                        for i in range(FT):
                            dve.wait_ge(f_h, r * FT + (i + 1 + CR))
                            dve.wait_ge(f_hm, r * FT + (i - 1 + CR))
                            ba, bg = FH[i % 2]
                            nc.vector.scalar_tensor_tensor(out=hg[:, i % 2, :], in0=bg[:, 0:F], scalar=rsf[:, slot, i:i + 1],
                                                           in1=bias1[:, F:2 * F], op0=ALU.mult, op1=ALU.add)
                            nc.vector.scalar_tensor_tensor(out=ha[:, i % 2, :], in0=ba[:, 0:F], scalar=rsf[:, slot, i:i + 1],
                                                           in1=bias1[:, 0:F], op0=ALU.mult, op1=ALU.add).then_inc(f_hb, 1)
                        dve.wait_ge(f_z, r + (1 + CR))
                        dve.wait_ge(f_xs, k + (1 + CR))
                        nc.vector.tensor_tensor(x[:, bass.ds((f * 2 + slot) * FT + 1, FT), :], FZ[:].rearrange("p (t d) -> p t d", t=FT),
                                                xbf[:, slot], ALU.add).then_inc(x_full, 2)
            dve.wait_ge(x_full, (DEPTH + 1) * B)
            for i in range(4):
                xv = x[:, 1 + i * NT // 4:1 + (i + 1) * NT // 4, :].rearrange("p (b t) d -> p b t d", t=TPB)
                nc.vector.tensor_tensor(xv, xv, gb[:, i * B // 4:(i + 1) * B // 4, None, :].to_broadcast([P, B // 4, TPB, D]),
                                        ALU.mult).then_inc(scaled, 1)
            for i in range(4):
                part = slice(i * NT // 4, (i + 1) * NT // 4)
                xo = x[:, 1 + i * NT // 4:1 + (i + 1) * NT // 4, :]
                dve.wait_ge(scaled, i + 1)
                nc.vector.tensor_tensor(xo, xo, x1[:, part, :], ALU.add).then_inc(gated, 1)

        @block.tensor
        def _(pe):
            for s in (xT_done, chunk_done, rot_turned, sims_done, pt_done, pv_done, wo_done,
                      w1c_mm, bias_mm, f_xT, f_yc, f_h, f_hT, f_z):
                pe.sem_inc(s, CR)
            mm = nc.tensor.matmul
            pe.wait_ge(const_in, 16 * N_CONST)
            pe.wait_ge(dve_setup, 10)
            pe.wait_ge(pool_setup, POOL_SETUP)
            nc.tensor.transpose(bank[0][:, 0:B], crow[:], ident[0:B, 0:B]).then_inc(pe_setup, 1)

            with pe.Fori(0, B) as b:
                pe.wait_ge(m_dve, b * DA + 1)
                mm(bank[0][:, 0:3 * D], cb_l[:], wmod_s[:, 0:3 * D], start=True, stop=True)
                mm(bank[1][:, 0:3 * D], cb_l[:], wmod_s[:, 3 * D:6 * D], start=True, stop=True).then_inc(m_pe, 1)
                pe.wait_ge(m_dve, b * DA + 12)
                for t in range(TPB):
                    last = nc.tensor.transpose(bank[2][:, t * P:(t + 1) * P], h1s[:, t, :], ident[:])
                last.then_inc(m_pe, 1)
                pe.wait_ge(m_act, b * AA + 4)
                mm(bank[3][:, 0:S], w1q[:], h1T[:], start=True, stop=True)
                mm(bank[4][:, 0:S], w1k[:], h1T[:], start=True, stop=True)
                for t in range(TPB):
                    last = mm(bank[5][:, t * D:(t + 1) * D], h1T[:, t * P:(t + 1) * P], w1v[:], start=True, stop=True)
                last.then_inc(m_pe, 1)
                pe.wait_ge(m_act, b * AA + 6)
                for q, k, at in ((0, 0, 0), (1, 0, 1), (1, 1, 2)):
                    o = bank[6][:, at * P:(at + 1) * P]
                    if q == k:
                        mm(o, identb[:], mask_causal, start=True, stop=False)
                    last = mm(o, q1T[:, q * P:(q + 1) * P], k1T[:, k * P:(k + 1) * P], start=(q != k), stop=True)
                last.then_inc(m_pe, 1)
                pe.wait_ge(m_dve, b * DA + 19)
                for i in range(3):
                    last = nc.tensor.transpose(bank[7][:, i * P:(i + 1) * P], p1[:, i * P:(i + 1) * P], ident[:])
                last.then_inc(m_pe, 1)
                pe.wait_ge(m_act, b * AA + 9)
                mm(bank[0][:, 0:P], v1[:, 0, :], p1T[:, 0:P], start=True, stop=True)
                mm(bank[0][:, P:S], v1[:, 0, :], p1T[:, P:2 * P], start=True, stop=False)
                mm(bank[0][:, P:S], v1[:, 1, :], p1T[:, 2 * P:3 * P], start=False, stop=True).then_inc(m_pe, 1)
                pe.wait_ge(m_act, b * AA + 10)
                for t in range(TPB):
                    last = mm(bank[1][:, t * D:(t + 1) * D], o1T[:, t * P:(t + 1) * P], w1o[:], start=True, stop=True)
                last.then_inc(m_pe, 1)

            def x_turn(a, y, done):
                pe.wait_ge(xs_ready, y + (1 + CR))
                pe.wait_ge(t_copied, a * KQ + (done + CR))
                nc.tensor.transpose(T[:, 0:P], xs[:], ident[:]).then_inc(xT_done, 1)

            def chunk(a, y, c, par):
                if c == 0:
                    pe.wait_ge(yT_ready, y + (1 + CR))
                if c < 2:
                    pe.wait_ge(v_done, a * 2 + (c - 1 + CR))
                else:
                    pe.wait_ge(prod_done, a * KQ + (c - 1 + CR))
                mm(G[c % 2][:], yT[:, par * P:(par + 1) * P], wqkv[:, CHUNK_COL[c]:CHUNK_COL[c] + CH],
                   start=True, stop=True).then_inc(chunk_done, 1)

            def turn(a, c):
                pe.wait_ge(rot_done, a * KQ + (c + 1 + CR))
                pe.wait_ge(t_copied, a * KQ + (c + CR))
                for i in range(4):
                    last = nc.tensor.transpose(T[:, i * P:(i + 1) * P], rot[:, c % 2, i * P:(i + 1) * P], ident[:])
                last.then_inc(rot_turned, 1)

            def sims(g, a, s, par, batch):
                if s == 0:
                    pe.wait_ge(t_copied, a * KQ + (2 + CR))
                    if par:
                        pe.wait_ge(ktail_done, batch + (1 + CR))
                if s == 4:
                    pe.wait_ge(t_copied, a * KQ + (4 + CR))
                pe.wait_ge(exp_done, g + (s - 1 + CR))
                N = WIDE if par else P
                kT, mask = (kTo, mask_odd) if par else (kTe, mask_even)
                bk = SIM[s % 2]
                mm(bk[:, 0:2 * N].rearrange("p (h n) -> p h n", h=2), identb[:], mask[:, None, :].to_broadcast([P, 2, N]),
                   start=True, stop=False, skip_group_check=True)
                for h in range(2):
                    last = mm(bk[:, h * N:(h + 1) * N], qT[:, par, h, s, :], kT[:, s, :], start=False, stop=(h == 1),
                              skip_group_check=True)
                last.then_inc(sims_done, 1)

            def p_turn(g, s, par):
                pe.wait_ge(norm_done, g + (s + 1 + CR))
                pe.wait_ge(pt_copied, g + (s + CR))
                slot = s % 2
                own = WIN if par else 0
                for h in range(2):
                    last = nc.tensor.transpose(PT[:, h * P:(h + 1) * P], pr[:, slot, h, own:own + P], ident[:])
                if par:
                    for h in range(2):
                        last = nc.tensor.transpose(PT[0:WIN, 2 * P + h * WIN:2 * P + (h + 1) * WIN], pr[0:WIN, slot, h, 0:WIN],
                                                   ident[0:WIN, 0:WIN])
                last.then_inc(pt_done, 1)

            def outputs(b, g, a, s, par, batch):
                pe.wait_ge(pt_copied, g + (s + 1 + CR))
                if s == 0:
                    pe.wait_ge(v_done, a * 2 + (1 + CR))
                    if par:
                        pe.wait_ge(vtail_done, batch * 16 + 16)
                if s == 4:
                    pe.wait_ge(v_done, a * 2 + (2 + CR))
                if s % 4 == 0:
                    pe.wait_ge(o_copied, b * 2 + (s // 4 + CR))
                slot, col = s % 2, (s % 4) * P
                for h in range(2):
                    head = slice((2 * s + h) * DH, (2 * s + h + 1) * DH)
                    half = slice(h * DH, (h + 1) * DH)
                    last = mm(O[half, col:col + P], v[:, par, head], pT[:, slot, h * P:(h + 1) * P], start=True, stop=not par,
                              skip_group_check=True)
                    if par:
                        last = mm(O[half, col:col + WIN], vt[:, head], pT[0:WIN, slot, 2 * P + h * WIN:2 * P + (h + 1) * WIN],
                                  start=False, stop=True, skip_group_check=True)
                last.then_inc(pv_done, 1)

            def project(b, w):
                pe.wait_ge(o_copied, b * 2 + CR)
                pe.wait_ge(x_upd, w + CR)
                for c in range(PAIRS):
                    last = mm(Z[:, 0:D], oT[:, c, :], wo[:, c, :], start=(c == 0), stop=(c == PAIRS - 1))
                last.then_inc(wo_done, 1)

            def tile(b, a, y, w, par, batch):
                g = b * PAIRS
                nxt = 1 - par
                sims(g, a - 1, 0, par, batch)
                sims(g, a - 1, 1, par, batch)
                project(b, w)
                for s in range(PAIRS):
                    if s + 2 < PAIRS:
                        sims(g, a - 1, s + 2, par, batch)
                    if s < KQ:
                        chunk(a, y, s, nxt)
                    p_turn(g, s, par)
                    if s == 0:
                        pe.wait_ge(yT_ready, y + (1 + CR))
                    if s < 2:
                        turn(a - 1, s + 2)
                    if s == 4:
                        turn(a, 0)
                    if s == 5:
                        chunk(a, y, 4, nxt)
                    if s == 6:
                        turn(a, 1)
                    if s >= 1:
                        outputs(b, g, a - 1, s - 1, par, batch)
                chunk(a, y, 5, nxt)
                x_turn(a, y + 1, 2)
                outputs(b, g, a - 1, PAIRS - 1, par, batch)

            with pe.Fori(0, DEPTH) as L:
                pe.wait_ge(x_full, (L + 1) * B)
                pe.wait_ge(attn_w_in, (L + 1) * (16 * N_ATTN))
                x_turn(L * AT, L * YT, 0)
                for c in range(6):
                    chunk(L * AT, L * YT, c, 0)
                for c in range(2):
                    turn(L * AT, c)
                x_turn(L * AT, L * YT + 1, 2)
                with pe.Fori(0, B) as j:
                    for par in range(2):
                        t = j * 2 + par
                        tile(L * NT + t, L * AT + t + 1, L * YT + t + 1, L * (NT + 1) + t, par, L * B + j)
                project((L + 1) * NT, L * (NT + 1) + NT)
                pe.wait_ge(yT_ready, (L + 1) * YT + CR)
                for c in range(2, KQ):
                    turn(L * AT + NT, c)
                pe.wait_ge(x_upd, (L + 1) * (NT + 1) + CR)
                pe.wait_ge(v_done, (L + 1) * (2 * AT) + CR)
                pe.wait_ge(t_copied, (L + 1) * (KQ * AT) + CR)
                pe.wait_ge(w1g_done, L + (1 + CR))
                for i in range(2):
                    last = mm(bank[i][:, 0:F], center[:], w1g[:, i * F:(i + 1) * F], start=True, stop=True)
                last.then_inc(w1c_mm, 1)
                for i in range(2):
                    last = mm(bank[5 + i][:, 0:F], lnb_l[:], w1[:, i * F:(i + 1) * F], start=True, stop=True)
                last.then_inc(bias_mm, 1)
                pe.wait_ge(w1c_done, L + (1 + CR))
                pe.wait_ge(bias_done, L + (1 + CR))

                def x_turns(k):
                    pe.wait_ge(f_xs, k + (1 + CR))
                    for i in range(FT):
                        last = nc.tensor.transpose(FT_B[:, i * P:(i + 1) * P], xsf[:, i, :], ident[:])
                    last.then_inc(f_xT, 1)

                def centred_rows(k, slot):
                    pe.wait_ge(f_yT, k + (1 + CR))
                    pe.wait_ge(f_ss, k * FT + CR)
                    for i in range(FT):
                        last = mm(FYC[:, i * P:(i + 1) * P], yTf[:, slot, i // TPB, (i % TPB) * P:(i % TPB + 1) * P], center[:],
                                  start=True, stop=True)
                    last.then_inc(f_yc, 1)

                def hidden(m, slot, i):
                    pe.wait_ge(f_hb, m + (i - 1 + CR))
                    for half in (1, 0):
                        last = mm(FH[i % 2][half][:, 0:F], yTf[:, slot, i // TPB, (i % TPB) * P:(i % TPB + 1) * P],
                                  w1c[:, half * F:(half + 1) * F], start=True, stop=True)
                    last.then_inc(f_h, 1)

                x_turns(L * (NF + 1))
                centred_rows(L * (NF + 1), 0)
                with pe.Fori(0, NF // 2) as f:
                    for slot in range(2):
                        k = L * (NF + 1) + f * 2 + slot
                        m = (L * NF + f * 2 + slot) * FT
                        hidden(m, slot, 0)
                        hidden(m, slot, 1)
                        x_turns(k + 1)
                        for i in range(FT):
                            pe.wait_ge(f_hm, m + (i + 1 + CR))
                            pe.wait_ge(f_hTc, m + (i + CR))
                            for c, (at, size) in enumerate(FCH):
                                last = nc.tensor.transpose(FHT[0:size, c * P:(c + 1) * P], hm[:, i % 2, at:at + size], ident[:])
                            last.then_inc(f_hT, 1)
                            if i + 2 < FT:
                                hidden(m, slot, i + 2)
                            if i == 0:
                                centred_rows(k + 1, 1 - slot)
                            pe.wait_ge(f_hTc, m + (i + 1 + CR))
                            if i == 0:
                                pe.wait_ge(x_full, (L + 1) * B + (f * 2 + slot) * 2)
                            for c, (at, size) in enumerate(FCH):
                                last = mm(FZ[:, i * D:(i + 1) * D], hT[0:size, i % 2, c * P:(c + 1) * P], w2[0:size, c, :],
                                          start=(c == 0), stop=(c == 2))
                        last.then_inc(f_z, 1)


def _constants():
    f32 = np.float32
    ident = np.eye(P, dtype=f32)
    q = np.arange(P)[:, None]
    even = np.arange(P)[None, :]
    odd = np.arange(WIDE)[None, :] - WIN
    band = lambda k: np.where((k > q) | (k < q - WIN), f32(MASKED), f32(0))
    masks = np.concatenate([band(even), band(odd), np.where(even > q, f32(MASKED), f32(0))], 1).astype(f32)
    center = (ident - f32(1.0 / D)).astype(f32)
    half = np.arange(0, DH, 2, dtype=f32)
    inv_freq = f32(1.0) / np.power(f32(10000.0), half / f32(DH), dtype=f32)
    t = np.arange(S, dtype=f32)
    freqs = t[:, None] * inv_freq[None, :]
    freqs = np.concatenate([freqs, freqs], -1)
    base = (half + f32(0.4 * DH)) / f32(1.4 * DH)
    power = (t - f32(S // 2)) / f32(WIN // 2)
    scale = np.power(base[None, :], power[:, None], dtype=f32)
    scale = np.concatenate([scale, scale], -1)
    sign = np.where(np.arange(DH) < DH // 2, f32(-1), f32(1))
    cos, sin = np.cos(freqs).astype(f32), np.sin(freqs).astype(f32) * sign
    inv = f32(1.0) / scale
    rope = np.stack([cos * inv, sin * inv, cos * scale * f32(QK_SCALE), sin * scale * f32(QK_SCALE)], 0)
    rope = rope.reshape(4, TPB, P, DH).transpose(2, 0, 1, 3)
    return {"ident": ident, "masks": masks, "center": center, "rope": np.ascontiguousarray(rope.astype(f32))}


_INS = ['L0_attn_x', 'L0_attn_Wq', 'L0_attn_Wk', 'L0_attn_Wv', 'L0_attn_Wo', 'L0_ffn_Wqkv', 'L0_ffn_q_scale',
        'L0_ffn_k_scale', 'L0_ffn_Wo', 'L0_ffn_ln_g', 'L0_ffn_ln_b', 'L0_ffn_W1', 'L0_ffn_b1', 'L0_ffn_W2',
        'L0_ffn_b2', 'L0_c', 'L0_wmod']


def kernel(**inputs):
    import concourse.bacc as bacc
    from concourse.bass_utils import run_bass_kernel_spmd as run

    nc = bacc.Bacc("TRN2", target_bir_lowering=False, num_devices=1)
    arrays, args = {}, []
    named = [(n, np.ascontiguousarray(inputs[n])) for n in _INS] + list(_constants().items())
    for name, a in named:
        arrays[f"in_{name}"] = a
        args.append(nc.dram_tensor(f"in_{name}", a.shape, mybir.dt.from_np(a.dtype), kind="ExternalInput").ap())
    args.append(nc.dram_tensor("out_0", (B, S, D), F32, kind="ExternalOutput").ap())
    build(nc, *args)
    r = run(nc, [arrays], core_ids=[0])
    return r.results[0]["out_0"]
```

```python
from contextlib import ExitStack

import numpy as np
import concourse.bass as bass
from concourse import mybir

F32 = mybir.dt.float32
BF16 = mybir.dt.bfloat16
ACT = mybir.ActivationFunctionType
ALU = mybir.AluOpType
AX = mybir.AxisListType

P = 128
D = 128
B, S = 16, 256
TPB = S // P
NT = B * TPB
DEPTH = 6
H, DH = 16, 64
INNER = H * DH
PAIRS = H // 2
WIN = 32
WIDE = WIN + P
F = 341
FCH = [(0, 128), (128, 128), (256, 85)]
HPC = 8
CH = HPC * DH
KQ = 4
AT = NT + 1
YT = NT + 2
ST = NT * PAIRS + 2
OT = 2 * NT + 1
FT = 4
NF = NT // FT
MASKED = -1.0e25
EPS = 1e-5
RMS_SCALE = float(D) ** -0.5
POOL_SETUP = 9
QK_SCALE = 8.0
ATT1_SCALE = float(D) ** -0.5
CR = 4
CHUNK_COL = [0, INNER, CH, INNER + CH, 2 * INNER, 2 * INNER + CH]


def build(nc, a_x, a_wq, a_wk, a_wv, a_wo, f_wqkv, f_qs, f_ks, f_wo, f_g, f_b, f_w1, f_b1, f_w2, f_b2,
          c_in, wmod, ident_in, masks_in, center_in, rope_in, out):
    with ExitStack() as ctx:
        def sb(name, shape, dt=F32):
            return ctx.enter_context(nc.sbuf_tensor(name, shape, dt))

        def sem(name):
            return ctx.enter_context(nc.semaphore(name))

        bank = [ctx.enter_context(nc.psum_tensor(f"bank{i}", [P, 512], F32)) for i in range(8)]

        ident = sb("ident", [P, P])
        identb = sb("identb", [P, P], BF16)
        mask_f = sb("mask_f", [P, P + WIDE + P])
        masks = sb("masks", [P, P + WIDE + P], BF16)
        mask_even, mask_odd, mask_causal = masks[:, 0:P], masks[:, P:P + WIDE], masks[:, P + WIDE:]
        center = sb("center", [P, P])
        rope = sb("rope", [P, 4, TPB, DH])
        neg_half = sb("neg_half", [P, HPC])
        eps = sb("eps", [P, HPC])
        x = sb("x", [P, 1 + NT + FT, D])
        x1 = sb("x1", [P, NT, D])
        gb = sb("gb", [P, B, D])
        w1q, w1k, w1v, w1o = (sb(f"w1{n}", [P, D]) for n in "qkvo")
        wmod_s = sb("wmod_s", [P, 6 * D])
        crow = sb("crow", [B, D])
        cT = sb("cT", [P, B])
        csig = sb("csig", [P, B])
        cden = sb("cden", [P, B])
        cinv = sb("cinv", [P, B])
        csilu = sb("csilu", [P, B])
        cb_l = sb("cb_l", [P, P])
        mod = sb("mod", [P, 6, D])
        gate_sign = sb("gate_sign", [P, 2, D])
        gate_pos = sb("gate_pos", [P, 2, D])
        gate_abs = sb("gate_abs", [P, 2, D])
        tsum = [sb(f"tsum{u}", [P, TPB]) for u in range(2)]
        nmean = [sb(f"nmean{u}", [P, TPB]) for u in range(2)]
        xc = sb("xc", [P, TPB, D])
        sqj = sb("sqj", [P, TPB, D])
        ssq = [sb(f"ssq{u}", [P, TPB]) for u in range(2)]
        var1 = [sb(f"var1{u}", [P, TPB]) for u in range(2)]
        rstd = [sb(f"rstd{u}", [P, TPB]) for u in range(2)]
        h1 = sb("h1", [P, TPB, D])
        h1s = sb("h1s", [P, TPB, D])
        ga = sb("ga", [P, D])
        xn = sb("xn", [P, TPB, D])
        h1T = sb("h1T", [P, S])
        q1T = sb("q1T", [P, S])
        k1T = sb("k1T", [P, S])
        v1 = sb("v1", [P, TPB, D])
        nm1 = [sb(f"nm1{u}", [P, TPB]) for u in range(2)]
        nms1 = [sb(f"nms1{u}", [P, TPB]) for u in range(2)]
        sum1 = [sb(f"sum1{u}", [P, TPB]) for u in range(2)]
        rin1 = [sb(f"rin1{u}", [P, TPB]) for u in range(2)]
        p1 = sb("p1", [P, P + S])
        p1T = sb("p1T", [P, 3 * P])
        o1T = sb("o1T", [P, S])
        att1 = sb("att1", [P, TPB, D])
        wqkv = sb("wqkv", [P, 3 * INNER])
        wo = sb("wo", [P, PAIRS, D])
        scales = sb("scales", [P, 2, DH])
        tables = sb("tables", [P, 4, TPB, DH])
        w1 = sb("w1", [P, 2 * F])
        w1g = sb("w1g", [P, 2 * F])
        w1c = sb("w1c", [P, 2 * F])
        w2 = sb("w2", [P, 3, D])
        lng = sb("lng", [P, 1])
        lnb = sb("lnb", [P, 1])
        lnb_l = sb("lnb_l", [P, P])
        b1r = sb("b1r", [P, 2 * F])
        b2r = sb("b2r", [P, D])
        bias1 = sb("bias1", [P, 2 * F])
        xs = sb("xs", [P, D])
        yT = sb("yT", [P, 2, P + 1])
        sq = sb("sq", [P, 2, CH])
        rc = sb("rc", [P, 2, CH])
        rs = sb("rs", [P, 2, CH])
        rsq = sb("rsq", [P, 2, CH])
        rsk = sb("rsk", [P, CH])
        rot = sb("rot", [P, 2, CH])
        n2 = sb("n2", [P, KQ, HPC])
        n2g = sb("n2g", [P, KQ, HPC])
        rn = sb("rn", [P, 2, KQ, HPC])
        qT = sb("qT", [P, 2, 2, PAIRS, P])
        kTe = sb("kTe", [P, PAIRS, P])
        kTo = sb("kTo", [P, PAIRS, WIDE])
        v = sb("v", [P, 2, INNER])
        vt = sb("vt", [WIN, INNER])
        nmax = sb("nmax", [P, 2, 2])
        shift = sb("shift", [P, 2, 2])
        psm = sb("psm", [P, 2, 2])
        pinv = sb("pinv", [P, 2, 2])
        pr = sb("pr", [P, 2, 2, WIDE])
        pT = sb("pT", [P, 2, 2 * P + 2 * WIN])
        oT = sb("oT", [P, PAIRS, P])
        xsf = sb("xsf", [P, FT, D])
        xbf = sb("xbf", [P, 2, FT, D])
        yTf = sb("yTf", [P, 2, FT // TPB, S + 1])
        sqf = sb("sqf", [P, FT, D])
        ssf = sb("ssf", [P, FT])
        vaf = sb("vaf", [P, FT])
        rsf = sb("rsf", [P, 2, FT])
        ha = sb("ha", [P, 2, F])
        hg = sb("hg", [P, 2, F])
        gg = sb("gg", [P, 2, F])
        hm = sb("hm", [P, 2, F])
        warm = sb("warm", [P, 1])
        hT = sb("hT", [P, 2, 3 * P])

        def lend(buf, *shapes):
            flat, at = buf[:].rearrange("p a b -> p (a b)"), 0
            for shape in shapes:
                size = int(np.prod(shape))
                view = flat[:, at:at + size]
                at += size
                yield view.rearrange("p (a b) -> p a b", b=shape[1]) if len(shape) == 2 else view

        mod_b, gate_sign_b, gate_pos_b, gate_abs_b, p1_b, cb_l_b = lend(v, (6, D), (2, D), (2, D), (2, D), (P + S,), (P,))
        mod, gate_sign, gate_pos, gate_abs, p1, cb_l = ([mod[:], mod_b], [gate_sign[:], gate_sign_b], [gate_pos[:], gate_pos_b], [gate_abs[:], gate_abs_b], [p1[:], p1_b], [cb_l[:], cb_l_b])
        xc_b, sqj_b, h1_b, h1s_b = lend(rc, (TPB, D), (TPB, D), (TPB, D), (TPB, D))
        xc, sqj, h1, h1s = ([xc[:], xc_b], [sqj[:], sqj_b], [h1[:], h1_b], [h1s[:], h1s_b])
        xn_b, h1T_b, q1T_b, k1T_b = lend(rs, (TPB, D), (S,), (S,), (S,))
        xn, h1T, q1T, k1T = ([xn[:], xn_b], [h1T[:], h1T_b], [q1T[:], q1T_b], [k1T[:], k1T_b])
        v1_b, o1T_b, att1_b, ga_b = lend(sq, (TPB, D), (S,), (TPB, D), (D,))
        v1, o1T, att1, ga = ([v1[:], v1_b], [o1T[:], o1T_b], [att1[:], att1_b], [ga[:], ga_b])
        p1T_b, = lend(rsq, (3 * P,))
        p1T, = ([p1T[:], p1T_b],)

        const_in, out_done, attn_w_in, ffn_w_in = (sem(n) for n in ("const_in", "out_done", "attn_w_in", "ffn_w_in"))
        pool_setup, dve_setup, pe_setup, act_setup = (sem(n) for n in ("pool_setup", "dve_setup", "pe_setup", "act_setup"))
        m_act, m_dve, m_pe, m_pool = ([sem(f"{n}{u}") for u in range(2)] for n in ("m_act", "m_dve", "m_pe", "m_pool"))
        x_full = sem("x_full")
        tables_done = sem("tables_done")
        xs_ready, xT_done, yT_ready = (sem(n) for n in ("xs_ready", "xT_done", "yT_ready"))
        chunk_done, sq_done, prod_done, red_done = (sem(n) for n in ("chunk_done", "sq_done", "prod_done", "red_done"))
        rsum_done, guard_done, rn_done, rot_done = (sem(n) for n in ("rsum_done", "guard_done", "rn_done", "rot_done"))
        rot_turned, t_copied, v_done = (sem(n) for n in ("rot_turned", "t_copied", "v_done"))
        ktail_done, vtail_done = sem("ktail_done"), sem("vtail_done")
        sims_done, max_done, shift_done, exp_done, inv_done, norm_done = (
            sem(n) for n in ("sims_done", "max_done", "shift_done", "exp_done", "inv_done", "norm_done"))
        pt_done, pt_copied, pv_done, o_copied, wo_done, x_upd = (
            sem(n) for n in ("pt_done", "pt_copied", "pv_done", "o_copied", "wo_done", "x_upd"))
        w1g_done, w1c_mm, w1c_done, bias_mm, bias_done = (
            sem(n) for n in ("w1g_done", "w1c_mm", "w1c_done", "bias_mm", "bias_done"))
        f_xs, f_xT, f_yT, f_yc, f_ss, f_var, f_rstd = (
            sem(n) for n in ("f_xs", "f_xT", "f_yT", "f_yc", "f_ss", "f_var", "f_rstd"))
        f_xb = sem("f_xb")
        f_h, f_hb, f_gelu, f_hm, f_hT, f_hTc, f_z = (
            sem(n) for n in ("f_h", "f_hb", "f_gelu", "f_hm", "f_hT", "f_hTc", "f_z"))
        scaled, gated = sem("scaled"), sem("gated")

        G = [bank[0], bank[1]]
        T = bank[2]
        SIM = [bank[3], bank[4]]
        PT = bank[5]
        O = bank[6]
        Z = bank[7]
        FH = [(bank[5], bank[6]), (bank[0], bank[1])]
        FT_B, FYC, FHT, FZ = bank[2], bank[3], bank[4], bank[7]

        N_CONST, N_ATTN, N_FFN = 12, 4, 7
        DA, AA, PA, GA = 26, 12, 7, 4

        def settle(eng):
            eng.wait_ge(pool_setup, POOL_SETUP)

        block = ctx.enter_context(nc.Block())

        @block.sync
        def _(sp):
            x_dram = a_x.rearrange("b (t p) d -> p (b t) d", p=P)
            o_dram = out.rearrange("b (t p) d -> p (b t) d", p=P)
            for dst, src in ((crow[:], c_in), (ident[:], ident_in), (wmod_s[:], wmod), (mask_f[:], masks_in),
                             (w1q[:], a_wq), (w1k[:], a_wk), (w1v[:], a_wv), (w1o[:], a_wo),
                             (center[:], center_in), (rope[:], rope_in)):
                sp.dma_start(dst, src).then_inc(const_in, 16)
            for i in range(2):
                half = slice(i * NT // 2, (i + 1) * NT // 2)
                sp.dma_start(x1[:, half, :], x_dram[:, half, :]).then_inc(const_in, 16)
            with sp.Fori(0, DEPTH) as L:
                sp.wait_ge(v_done, L * (2 * AT) + CR)
                sp.wait_ge(prod_done, L * (KQ * AT) + CR)
                sp.wait_ge(x_upd, L * (NT + 1) + CR)
                sp.dma_start(wqkv[:], f_wqkv[bass.ds(L, 1)].rearrange("l p n -> p (l n)")).then_inc(attn_w_in, 16)
                sp.dma_start(wo[:], f_wo[bass.ds(L, 1)].rearrange("l (c p) n -> p (l c) n", p=P)).then_inc(attn_w_in, 16)
                sp.dma_start(scales[:, 0, :], f_ks[bass.ds(L, 1)].to_broadcast([P, DH])).then_inc(attn_w_in, 16)
                sp.dma_start(scales[:, 1, :], f_qs[bass.ds(L, 1)].to_broadcast([P, DH])).then_inc(attn_w_in, 16)
                sp.wait_ge(x_full, (L + 1) * B)
                sp.dma_start(w1[:], f_w1[bass.ds(L, 1)].rearrange("l p n -> p (l n)")).then_inc(ffn_w_in, 16)
                sp.dma_start(w2[:, 0:2, :], f_w2[bass.ds(L, 1), 0:2 * P].rearrange("l (c p) n -> p (l c) n", p=P)).then_inc(ffn_w_in, 16)
                sp.dma_start(w2[0:F - 2 * P, 2, :], f_w2[bass.ds(L, 1), 2 * P:F].rearrange("l p n -> p (l n)")).then_inc(ffn_w_in, 16)
                sp.dma_start(lng[:], f_g[bass.ds(L, 1)].rearrange("l p -> p l")).then_inc(ffn_w_in, 16)
                sp.dma_start(lnb[:], f_b[bass.ds(L, 1)].rearrange("l p -> p l")).then_inc(ffn_w_in, 16)
                sp.dma_start(b1r[:], f_b1[bass.ds(L, 1)].to_broadcast([P, 2 * F])).then_inc(ffn_w_in, 16)
                sp.dma_start(b2r[:], f_b2[bass.ds(L, 1)].to_broadcast([P, D])).then_inc(ffn_w_in, 16)
                with sp.Fori(0, B) as j:
                    sp.wait_ge(v_done, (L * AT + j * 2) * 2 + (2 + CR))
                    sp.wait_ge(pv_done, (L * NT + j * 2) * PAIRS + CR)
                    sp.dma_start(vt[:], v[P - WIN:P, 0, :]).then_inc(vtail_done, 16)
            for i in range(4):
                part = slice(i * NT // 4, (i + 1) * NT // 4)
                sp.wait_ge(gated, i + 1)
                sp.dma_start(o_dram[:, part, :], x[:, 1 + i * NT // 4:1 + (i + 1) * NT // 4, :]).then_inc(out_done, 16)
            sp.wait_ge(out_done, 64)

        @block.gpsimd
        def _(pool):
            for s in (xs_ready, rsum_done, guard_done, rn_done, rot_done, f_var, f_rstd, f_hm):
                pool.sem_inc(s, CR)
            nc.gpsimd.memset(neg_half[:], -0.5).then_inc(pool_setup, 1)
            nc.gpsimd.memset(eps[:], EPS).then_inc(pool_setup, 1)
            nc.gpsimd.memset(x[:, 0, :], 0.0).then_inc(pool_setup, 1)
            nc.gpsimd.memset(x[:, NT + 1:, :], 0.0).then_inc(pool_setup, 1)
            nc.gpsimd.memset(oT[:], 0.0).then_inc(pool_setup, 1)
            nc.gpsimd.memset(yTf[:, :, :, 0:1], 0.0).then_inc(pool_setup, 1)
            nc.gpsimd.memset(yT[:, :, 0:1], 0.0).then_inc(pool_setup, 1)
            pool.wait_ge(pool_setup, POOL_SETUP - 2)
            nc.gpsimd.memset(qT[0:DH, :, 1], 0.0).then_inc(pool_setup, 1)
            pool.wait_ge(pool_setup, POOL_SETUP - 1)
            nc.gpsimd.memset(qT[DH:P, :, 0], 0.0).then_inc(pool_setup, 1)
            pool.wait_ge(pool_setup, POOL_SETUP)

            with pool.Fori(0, B // 2) as j:
                for half in range(2):
                    for u in range(2):
                        pool.wait_ge(m_act[u], j * AA + (3, AA)[half])
                        nc.gpsimd.tensor_tensor(var1[u][:], ssq[u][:], eps[:, 0:TPB], ALU.add).then_inc(m_pool[u], 1)
                        pool.wait_ge(m_pool[u], j * GA + (2 * half + 1))
                        nc.gpsimd.tensor_tensor(rstd[u][:], var1[u][:], neg_half[:, 0:TPB], ALU.pow).then_inc(m_pool[u], 1)

            def load_x(tile):
                nc.gpsimd.tensor_copy(xs[:], x[:, tile, :].rearrange("p a d -> p (a d)")).then_inc(xs_ready, 1)

            def rotary_sum(a, c):
                n = a * KQ + c
                pool.wait_ge(prod_done, n + (1 + CR))
                if c % 2 == 0:
                    pool.wait_ge(rot_turned, n + (CR - 3))
                nc.gpsimd.tensor_tensor(rsk[:] if c % 2 else rsq[:, c // 2, :], rc[:, c % 2, :], rs[:, c % 2, :], ALU.add).then_inc(rsum_done, 1)

            def norm_factor(a, c, par):
                settle(pool)
                pool.wait_ge(red_done, a * KQ + (c + 1 + CR))
                done = a * KQ + (c + (0 if c % 2 else 2) + CR)
                nc.gpsimd.tensor_scalar(n2g[:, c, :], n2[:, c, :], 1e-24, None, ALU.max).then_inc(guard_done, 1)
                pool.wait_ge(guard_done, done)
                nc.gpsimd.tensor_tensor(rn[:, par, c, :], n2g[:, c, :], neg_half[:], ALU.pow).then_inc(rn_done, 1)

            def rotate(a, following, par):
                for c in (0, 2):
                    rotary_sum(a, c)
                    if c == 0:
                        load_x(following)
                    rotary_sum(a, c + 1)
                    norm_factor(a, c + 1, par)
                    pool.wait_ge(rn_done, a * KQ + (c + 1 + CR))
                    pool.wait_ge(rot_turned, a * KQ + (c - 2 + CR))
                    nc.gpsimd.tensor_tensor(
                        rot[:, c // 2, :].rearrange("p (h d) -> p h d", d=DH),
                        rsk[:].rearrange("p (h d) -> p h d", d=DH),
                        rn[:, par, c + 1, :, None].to_broadcast([P, HPC, DH]), ALU.mult).then_inc(rot_done, 1)
                    norm_factor(a, c, par)

            with pool.Fori(0, DEPTH) as L:
                pool.wait_ge(attn_w_in, (L + 1) * (16 * N_ATTN))
                pool.wait_ge(x_full, (L + 1) * B)
                for i in range(4):
                    s = scales[:, i // 2, :].rearrange("p (x d) -> p x d", x=2)
                    if i % 2:
                        s = s[:, ::-1, :]
                    for t in range(TPB):
                        nc.gpsimd.tensor_tensor(
                            tables[:, i, t, :].rearrange("p (x d) -> p x d", x=2),
                            rope[:, i, t, :].rearrange("p (x d) -> p x d", x=2), s, ALU.mult).then_inc(tables_done, 1)
                load_x(bass.ds(1, 1))
                rotate(L * AT, bass.ds(2, 1), 0)
                with pool.Fori(0, B) as j:
                    for par in range(2):
                        rotate(L * AT + j * 2 + par + 1, bass.ds(j * 2 + par + 3, 1), 1 - par)
                def rstd_ffn(k, slot):
                    pool.wait_ge(f_ss, k * FT + (FT + CR))
                    nc.gpsimd.tensor_tensor(vaf[:], ssf[:], eps[:, 0:FT], ALU.add).then_inc(f_var, 1)
                    pool.wait_ge(f_var, k + (1 + CR))
                    nc.gpsimd.tensor_tensor(rsf[:, slot, :], vaf[:], neg_half[:, 0:FT], ALU.pow).then_inc(f_rstd, 1)

                rstd_ffn(L * (NF + 1), 0)
                with pool.Fori(0, NF // 2) as f:
                    for slot in range(2):
                        k = L * (NF + 1) + f * 2 + slot
                        m = (L * NF + f * 2 + slot) * FT
                        for i in range(FT):
                            pool.wait_ge(f_gelu, m + (i + 1 + CR))
                            pool.wait_ge(f_hT, m + (i - 1 + CR))
                            nc.gpsimd.tensor_tensor(hm[:, i % 2, :], ha[:, i % 2, :], gg[:, i % 2, :], ALU.mult).then_inc(f_hm, 1)
                            if i == 2:
                                rstd_ffn(k + 1, 1 - slot)

        @block.scalar
        def _(act):
            for s in (yT_ready, sq_done, t_copied, ktail_done, exp_done, pt_copied, o_copied,
                      w1c_done, f_yT, f_ss, f_gelu, f_hTc):
                act.sem_inc(s, CR)
            act.wait_ge(dve_setup, 11)
            nc.scalar.activation(csig[:], cT[:], ACT.Exp, scale=-1.0).then_inc(act_setup, 1)

            with act.Fori(0, B // 2) as j:
                for u in range(2):
                    act.wait_ge(m_pe[u], j * PA + 1)
                    nc.scalar.activation(mod[u][:, 0:3, :], bank[0 + 4 * u][:, 0:3 * D].rearrange("p (a d) -> p a d", d=D), ACT.Copy)
                    nc.scalar.activation(mod[u][:, 3:6, :], bank[1 + 4 * u][:, 0:3 * D].rearrange("p (a d) -> p a d", d=D), ACT.Copy).then_inc(m_act[u], 1)
                for u in range(2):
                    act.wait_ge(m_dve[u], j * DA + 4)
                    nc.scalar.activation(sqj[u][:, 0, :], xc[u][:, 0, :], ACT.Square, scale=RMS_SCALE, accum_out=ssq[u][:, 0:1]).then_inc(m_act[u], 1)
                    nc.scalar.activation(sqj[u][:, 1, :], xc[u][:, 1, :], ACT.Square, scale=RMS_SCALE, accum_out=ssq[u][:, 1:2]).then_inc(m_act[u], 1)
                for u in range(2):
                    act.wait_ge(m_pe[u], j * PA + 2)
                    nc.scalar.activation(h1T[u][:], bank[2 + 4 * u][:, 0:S], ACT.Copy).then_inc(m_act[u], 1)
                for u in range(2):
                    act.wait_ge(m_pe[u], j * PA + 3)
                    nc.scalar.activation(q1T[u][:], bank[3 + 4 * u][:, 0:S], ACT.Copy).then_inc(m_act[u], 1)
                    nc.scalar.activation(k1T[u][:], bank[0 + 4 * u][:, 0:S], ACT.Copy).then_inc(m_act[u], 1)
                for u in range(2):
                    act.wait_ge(m_dve[u], j * DA + 16)
                    nc.scalar.activation(p1[u][:, 0:P], bank[2 + 4 * u][:, 0:P], ACT.Exp, scale=ATT1_SCALE, bias=nms1[u][:, 0:1],
                                         accum_out=sum1[u][:, 0:1]).then_inc(m_act[u], 1)
                    nc.scalar.activation(p1[u][:, P:P + S], bank[2 + 4 * u][:, P:P + S], ACT.Exp, scale=ATT1_SCALE, bias=nms1[u][:, 1:2],
                                         accum_out=sum1[u][:, 1:2]).then_inc(m_act[u], 1)
                for u in range(2):
                    act.wait_ge(m_pe[u], j * PA + 5)
                    nc.scalar.activation(p1T[u][:], bank[3 + 4 * u][:, 0:3 * P], ACT.Copy).then_inc(m_act[u], 1)
                for u in range(2):
                    act.wait_ge(m_pe[u], j * PA + 6)
                    nc.scalar.activation(o1T[u][:], bank[0 + 4 * u][:, 0:S], ACT.Copy).then_inc(m_act[u], 1)
                for u in range(2):
                    act.wait_ge(m_dve[u], j * DA + 24)
                    nc.scalar.activation(sqj[u][:, 0, :], xc[u][:, 0, :], ACT.Square, scale=RMS_SCALE, accum_out=ssq[u][:, 0:1]).then_inc(m_act[u], 1)
                    nc.scalar.activation(sqj[u][:, 1, :], xc[u][:, 1, :], ACT.Square, scale=RMS_SCALE, accum_out=ssq[u][:, 1:2]).then_inc(m_act[u], 1)

            def exps(e, g, s, par):
                N = WIDE if par else P
                act.wait_ge(shift_done, e + (s + 1 + CR))
                act.wait_ge(pt_done, g + (s - 1 + CR))
                slot = s % 2
                for h in range(2):
                    c, col = (0 if s < 4 else 2), (2 * s + h) % HPC
                    last = nc.scalar.activation(pr[:, slot, h, 0:N], SIM[slot][:, h * N:(h + 1) * N], ACT.Exp,
                                                scale=rn[:, par, c, col:col + 1], bias=shift[:, slot, h:h + 1],
                                                accum_out=psm[:, slot, h:h + 1])
                last.then_inc(exp_done, 1)

            def pt_copy(g, s, par):
                act.wait_ge(pt_done, g + (s + 1 + CR))
                act.wait_ge(pv_done, g + (s - 1 + CR))
                n = 2 * P + (2 * WIN if par else 0)
                nc.scalar.activation(pT[:, s % 2, 0:n], PT[:, 0:n], ACT.Copy).then_inc(pt_copied, 1)

            def o_copy(pairs, u, w, half):
                act.wait_ge(pv_done, pairs + CR)
                act.wait_ge(wo_done, w + ((0 if half else 1) + CR))
                nc.scalar.activation(oT[:, 4 * half:4 * half + 4, :], O[:].rearrange("p (c t) -> p c t", c=4),
                                     ACT.Copy).then_inc(o_copied, 1)

            def y_copy(y, par):
                if par:
                    act.wait_ge(xT_done, y + (1 + CR))
                    act.wait_ge(yT_ready, y + CR)
                    nc.scalar.activation(yT[64:P, 1, 0:1], yT[64:P, 0, P:P + 1], ACT.Copy)
                else:
                    act.wait_ge(xT_done, y + (1 + CR))
                nc.scalar.activation(yT[0:64, par, 0:P], T[0:64, 0:P], ACT.Copy)
                nc.scalar.activation(yT[64:P, par, 1:P + 1], T[64:P, 0:P], ACT.Copy).then_inc(yT_ready, 1)

            def square(a, c):
                act.wait_ge(chunk_done, a * 6 + (c + 1 + CR))
                act.wait_ge(red_done, a * KQ + (c - 1 + CR))
                nc.scalar.activation(sq[:, c % 2, :], G[c % 2][:], ACT.Square).then_inc(sq_done, 1)

            def t_copy(a, c, par):
                act.wait_ge(rot_turned, a * KQ + (c + 1 + CR))
                half = slice(4 * (c // 2), 4 * (c // 2) + 4)
                src = T[:].rearrange("p (c t) -> p c t", c=4)
                if c % 2 == 0:
                    nc.scalar.activation(qT[0:DH, par, 0, half, :], src[0:DH], ACT.Copy)
                    nc.scalar.activation(qT[DH:P, par, 1, half, :], src[DH:P], ACT.Copy).then_inc(t_copied, 1)
                    return
                if par:
                    dst = kTo[:, half, WIN:WIDE]
                else:
                    dst = kTe[:, half, :]
                nc.scalar.activation(dst, src, ACT.Copy).then_inc(t_copied, 1)

            def tile(e, b, a, y, w, u, par):
                g = b * PAIRS
                nxt = 1 - par
                for s in range(PAIRS):
                    if s + 1 < PAIRS:
                        exps(e, g, s + 1, par)
                    else:
                        exps(e + PAIRS, g + PAIRS, 0, nxt)
                    if s == 0:
                        o_copy(g, u, w, 1)
                    if s == 5:
                        o_copy(g + 4, u + 1, w, 0)
                    pt_copy(g, s, par)
                    if s == 0:
                        square(a, 0)
                        t_copy(a - 1, 3, par)
                    if s == 1:
                        square(a, 1)
                    if s == 3:
                        y_copy(y + 1, par)
                        if nxt:
                            act.wait_ge(sims_done, e + (5 + CR))
                            nc.scalar.activation(kTo[:, :, 0:WIN], kTe[:, :, P - WIN:P], ACT.Copy).then_inc(ktail_done, 1)
                        square(a, 2)
                    if s == 4:
                        square(a, 3)
                        t_copy(a, 0, nxt)
                    if s == 5:
                        t_copy(a, 1, nxt)
                    if s == 7:
                        t_copy(a, 2, nxt)

            with act.Fori(0, DEPTH) as L:
                y_copy(L * YT, 0)
                for c in range(KQ):
                    square(L * AT, c)
                for c in range(2):
                    t_copy(L * AT, c, 0)
                y_copy(L * YT + 1, 1)
                t_copy(L * AT, 2, 0)
                exps(L * ST, L * (NT * PAIRS), 0, 0)
                with act.Fori(0, B) as j:
                    for par in range(2):
                        t = j * 2 + par
                        tile(L * ST + t * PAIRS, L * NT + t, L * AT + t + 1, L * YT + t + 1, L * (NT + 1) + t, L * OT + t * 2, par)
                exps(L * ST + NT * PAIRS, (L + 1) * (NT * PAIRS), 1, 0)
                t_copy(L * AT + NT, 3, 0)
                o_copy((L + 1) * (NT * PAIRS), (L + 1) * OT - 1, L * (NT + 1) + NT, 1)
                act.wait_ge(w1c_mm, L + (1 + CR))
                nc.scalar.activation(w1c[:, 0:F], bank[0][:, 0:F], ACT.Copy)
                nc.scalar.activation(w1c[:, F:2 * F], bank[1][:, 0:F], ACT.Copy).then_inc(w1c_done, 1)
                def front(k, slot):
                    act.wait_ge(f_xT, k + (1 + CR))
                    turned = FT_B[:].rearrange("p (b t) -> p b t", b=FT // TPB)
                    nc.scalar.activation(yTf[0:64, slot, :, 0:S], turned[0:64], ACT.Copy)
                    nc.scalar.activation(yTf[64:P, slot, :, 1:S + 1], turned[64:P], ACT.Copy).then_inc(f_yT, 1)

                def squares(k):
                    act.wait_ge(f_yc, k + (1 + CR))
                    for i in range(FT):
                        nc.scalar.activation(sqf[:, i, :], FYC[:, i * P:(i + 1) * P], ACT.Square, scale=RMS_SCALE,
                                             accum_out=ssf[:, i:i + 1]).then_inc(f_ss, 1)

                front(L * (NF + 1), 0)
                squares(L * (NF + 1))
                nc.scalar.activation(warm[:], eps[:, 0:1], ACT.Gelu)
                with act.Fori(0, NF // 2) as f:
                    for slot in range(2):
                        k = L * (NF + 1) + f * 2 + slot
                        m = (L * NF + f * 2 + slot) * FT
                        for i in range(FT + 1):
                            if i < FT:
                                act.wait_ge(f_hb, L * (NT + 1) + (f * 2 + slot) * FT + (i + 1 + CR))
                                act.wait_ge(f_hm, m + (i - 1 + CR))
                                nc.scalar.activation(gg[:, i % 2, :], hg[:, i % 2, :], ACT.Gelu).then_inc(f_gelu, 1)
                            if i == 1:
                                front(k + 1, 1 - slot)
                            if i == 2:
                                squares(k + 1)
                            if i >= 1:
                                act.wait_ge(f_hT, m + (i + CR))
                                nc.scalar.activation(hT[:, (i - 1) % 2, :], FHT[:, 0:3 * P], ACT.Copy).then_inc(f_hTc, 1)

        @block.vector
        def _(dve):
            for s in (red_done, prod_done, max_done, shift_done, inv_done, norm_done, v_done, x_upd, w1g_done, bias_done, f_xs, f_xb, f_hb):
                dve.sem_inc(s, CR)
            for i in range(8):
                nc.vector.memset(bank[i][:], 0.0).then_inc(dve_setup, 1)
            dve.wait_ge(const_in, 16 * N_CONST)
            nc.vector.tensor_copy(identb[:], ident[:]).then_inc(dve_setup, 1)
            nc.vector.tensor_copy(masks[:], mask_f[:]).then_inc(dve_setup, 1)
            dve.wait_ge(pe_setup, 1)
            nc.vector.tensor_copy(cT[:], bank[0][:, 0:B]).then_inc(dve_setup, 1)
            dve.wait_ge(act_setup, 1)
            nc.vector.tensor_scalar(cden[:], csig[:], 1.0, None, ALU.add).then_inc(dve_setup, 1)
            dve.wait_ge(dve_setup, 12)
            nc.vector.reciprocal(cinv[:], cden[:]).then_inc(dve_setup, 1)
            dve.wait_ge(dve_setup, 13)
            nc.vector.tensor_tensor(csilu[:], cT[:], cinv[:], ALU.mult).then_inc(dve_setup, 1)
            dve.wait_ge(dve_setup, 14)

            with dve.Fori(0, B // 2) as j:
                at = j * DA
                tiles = [bass.ds(j * (2 * TPB) + u * TPB, TPB) for u in range(2)]
                stream = [bass.ds(j * (2 * TPB) + (u * TPB + 1), TPB) for u in range(2)]

                def centred(u, first, src):
                    nc.vector.tensor_reduce(tsum[u][:], src, AX.X, ALU.add).then_inc(m_dve[u], 1)
                    dve.wait_ge(m_dve[u], at + first)
                    nc.vector.tensor_scalar(nmean[u][:], tsum[u][:], -1.0 / D, None, ALU.mult).then_inc(m_dve[u], 1)
                    dve.wait_ge(m_dve[u], at + (first + 1))
                    nc.vector.tensor_tensor(xc[u][:], src, nmean[u][:, :, None].to_broadcast([P, TPB, D]),
                                            ALU.add).then_inc(m_dve[u], 1)

                for u in range(2):
                    nc.vector.tensor_copy(cb_l[u][:], csilu[:, bass.ds(j * 2 + u, 1)].to_broadcast([P, P])).then_inc(m_dve[u], 1)
                    centred(u, 2, x1[:, tiles[u], :])
                for u in range(2):
                    dve.wait_ge(m_act[u], j * AA + 1)
                    nc.vector.tensor_scalar(mod[u][:, 1::3, :], mod[u][:, 1::3, :], 1.0, None, ALU.add)
                    nc.vector.tensor_scalar(gate_pos[u][:], mod[u][:, 2::3, :], 0.25, None, ALU.max).then_inc(m_dve[u], 1)
                    nc.vector.tensor_scalar(gate_sign[u][:], mod[u][:, 2::3, :], 0.0, 2.0, ALU.is_ge, ALU.mult).then_inc(m_dve[u], 1)
                    dve.wait_ge(m_dve[u], at + 5)
                    nc.vector.scalar_tensor_tensor(out=gate_abs[u][:], in0=mod[u][:, 2::3, :], scalar=-1.0, in1=gate_pos[u][:],
                                                   op0=ALU.mult, op1=ALU.max).then_inc(m_dve[u], 1)
                    dve.wait_ge(m_dve[u], at + 7)
                    nc.vector.scalar_tensor_tensor(out=ga[u][:], in0=gate_sign[u][:, 0, :], scalar=-1.0, in1=gate_abs[u][:, 0, :],
                                                   op0=ALU.add, op1=ALU.mult).then_inc(m_dve[u], 1)
                    nc.vector.scalar_tensor_tensor(out=gb[:, bass.ds(j * 2 + u, 1), :].rearrange("p a d -> p (a d)"), in0=gate_sign[u][:, 1, :],
                                                   scalar=-1.0, in1=gate_abs[u][:, 1, :], op0=ALU.add, op1=ALU.mult).then_inc(m_dve[u], 1)
                for u in range(2):
                    dve.wait_ge(m_pool[u], j * GA + 2)
                    for t in range(TPB):
                        nc.vector.scalar_tensor_tensor(out=h1[u][:, t, :], in0=xc[u][:, t, :], scalar=rstd[u][:, t:t + 1], in1=mod[u][:, 1, :],
                                                       op0=ALU.mult, op1=ALU.mult).then_inc(m_dve[u], 1)
                    dve.wait_ge(m_dve[u], at + 11)
                    nc.vector.tensor_tensor(h1s[u][:], h1[u][:], mod[u][:, 0:1, :].to_broadcast([P, TPB, D]), ALU.add).then_inc(m_dve[u], 1)
                for u in range(2):
                    dve.wait_ge(m_pe[u], j * PA + 3)
                    nc.vector.tensor_copy(v1[u][:], bank[1 + 4 * u][:, 0:S].rearrange("p (t d) -> p t d", t=TPB)).then_inc(m_dve[u], 1)
                for u in range(2):
                    dve.wait_ge(m_pe[u], j * PA + 4)
                    nc.vector.tensor_reduce(nm1[u][:, 0:1], bank[2 + 4 * u][:, 0:P], AX.X, ALU.max, negate=True).then_inc(m_dve[u], 1)
                    nc.vector.tensor_reduce(nm1[u][:, 1:2], bank[2 + 4 * u][:, P:P + S], AX.X, ALU.max, negate=True).then_inc(m_dve[u], 1)
                    dve.wait_ge(m_dve[u], at + 15)
                    nc.vector.tensor_scalar(nms1[u][:], nm1[u][:], ATT1_SCALE, None, ALU.mult).then_inc(m_dve[u], 1)
                for u in range(2):
                    dve.wait_ge(m_act[u], j * AA + 8)
                    nc.vector.reciprocal(rin1[u][:], sum1[u][:]).then_inc(m_dve[u], 1)
                    dve.wait_ge(m_dve[u], at + 17)
                    nc.vector.tensor_scalar(p1[u][:, 0:P], p1[u][:, 0:P], rin1[u][:, 0:1], None, ALU.mult).then_inc(m_dve[u], 1)
                    nc.vector.tensor_scalar(p1[u][:, P:P + S], p1[u][:, P:P + S], rin1[u][:, 1:2], None, ALU.mult).then_inc(m_dve[u], 1)
                for u in range(2):
                    dve.wait_ge(m_pe[u], j * PA + 7)
                    nc.vector.tensor_tensor(att1[u][:], bank[1 + 4 * u][:, 0:S].rearrange("p (t d) -> p t d", t=TPB),
                                            ga[u][:, None, :].to_broadcast([P, TPB, D]), ALU.mult).then_inc(m_dve[u], 1)
                    dve.wait_ge(m_dve[u], at + 20)
                    nc.vector.tensor_tensor(xn[u][:], x1[:, tiles[u], :], att1[u][:], ALU.add).then_inc(m_dve[u], 1)
                    dve.wait_ge(m_dve[u], at + 21)
                    centred(u, 22, xn[u][:])
                    nc.vector.tensor_copy(x1[:, tiles[u], :], xn[u][:])
                for u in range(2):
                    dve.wait_ge(m_pool[u], j * GA + 4)
                    for t in range(TPB):
                        nc.vector.scalar_tensor_tensor(out=h1[u][:, t, :], in0=xc[u][:, t, :], scalar=rstd[u][:, t:t + 1], in1=mod[u][:, 4, :],
                                                       op0=ALU.mult, op1=ALU.mult).then_inc(m_dve[u], 1)
                    dve.wait_ge(m_dve[u], at + 26)
                    nc.vector.tensor_tensor(x[:, stream[u], :], h1[u][:], mod[u][:, 3:4, :].to_broadcast([P, TPB, D]), ALU.add).then_inc(x_full, 1)

            def products(a, c, par):
                dve.wait_ge(sq_done, a * KQ + (c + 1 + CR))
                dve.wait_ge(rsum_done, a * KQ + (c - 1 + CR))
                slot, which = c % 2, 2 - 2 * (c % 2)
                nc.vector.tensor_tensor(rc[:, slot, :].rearrange("p (h d) -> p h d", d=DH),
                                        G[slot][:].rearrange("p (h d) -> p h d", d=DH),
                                        tables[:, which, par:par + 1, :].to_broadcast([P, HPC, DH]), ALU.mult)
                nc.vector.tensor_tensor(
                    rs[:, slot, :].rearrange("p (h x d) -> p h x d", x=2, d=DH // 2),
                    G[slot][:].rearrange("p (h x d) -> p h x d", x=2, d=DH // 2)[:, :, ::-1, :],
                    tables[:, which + 1, par:par + 1, :].to_broadcast([P, HPC, DH]).rearrange("p h (x d) -> p h x d", x=2),
                    ALU.mult).then_inc(prod_done, 1)

            def norms(a, c):
                dve.wait_ge(sq_done, a * KQ + (c + 1 + CR))
                nc.vector.tensor_reduce(n2[:, c, :], sq[:, c % 2, :].rearrange("p (h d) -> p h d", d=DH), AX.X,
                                        ALU.add).then_inc(red_done, 1)

            def maxima(e, s, par):
                N = WIDE if par else P
                dve.wait_ge(sims_done, e + (s + 1 + CR))
                nc.vector.tensor_reduce(nmax[:, s % 2, :], SIM[s % 2][:, 0:2 * N].rearrange("p (h n) -> p h n", h=2), AX.X,
                                        ALU.max, negate=True).then_inc(max_done, 1)

            def shifts(e, a, s, par):
                dve.wait_ge(max_done, e + (s + 1 + CR))
                if s % 4 == 0:
                    dve.wait_ge(rn_done, a * KQ + ((4 if s else 2) + CR))
                c, col = (0 if s < 4 else 2), (2 * s) % HPC
                nc.vector.tensor_tensor(shift[:, s % 2, :], nmax[:, s % 2, :], rn[:, par, c, col:col + 2],
                                        ALU.mult).then_inc(shift_done, 1)

            def inverses(e, s):
                dve.wait_ge(exp_done, e + (s + 1 + CR))
                nc.vector.reciprocal(pinv[:, s % 2, :], psm[:, s % 2, :]).then_inc(inv_done, 1)

            def normalise(e, s, par):
                N = WIDE if par else P
                slot = s % 2
                dve.wait_ge(inv_done, e + (s + 1 + CR))
                for h in range(2):
                    last = nc.vector.tensor_scalar(pr[:, slot, h, 0:N], pr[:, slot, h, 0:N], pinv[:, slot, h:h + 1], None, ALU.mult)
                last.then_inc(norm_done, 1)

            def update(w, at):
                dve.wait_ge(wo_done, w + (1 + CR))
                xt = x[:, at, :].rearrange("p a d -> p (a d)")
                nc.vector.tensor_tensor(xt, Z[:, 0:D], xt, ALU.add).then_inc(x_upd, 1)

            def v_copy(a, c, par):
                dve.wait_ge(chunk_done, a * 6 + (KQ + c + 1 + CR))
                nc.vector.tensor_copy(v[:, par, c * CH:(c + 1) * CH], G[c % 2][:]).then_inc(v_done, 1)

            def tile(e, a, w, par, at, batch):
                nxt = 1 - par
                chunk_of = {1: 0, 2: 1, 4: 2, 5: 3}
                steps = [(e, a - 1, s, par) for s in range(PAIRS)] + [(e + PAIRS, a, s, nxt) for s in range(2)]
                for s in range(PAIRS):
                    me, ma, ms, mp = steps[s + 2]
                    ne, _, ns, n_par = steps[s + 1]
                    maxima(me, ms, mp)
                    inverses(ne, ns)
                    shifts(me, ma, ms, mp)
                    normalise(ne, ns, n_par)
                    if s == 0:
                        v_copy(a - 1, 1, par)
                    if s == 3:
                        update(w, at)
                    if s == 6:
                        if not nxt:
                            dve.wait_ge(vtail_done, batch * 16 + 16)
                        v_copy(a, 0, nxt)
                    if s in chunk_of:
                        products(a, chunk_of[s], nxt)
                        norms(a, chunk_of[s])

            with dve.Fori(0, DEPTH) as L:
                dve.wait_ge(tables_done, L * 8 + 8)
                for c in range(KQ):
                    products(L * AT, c, 0)
                    norms(L * AT, c)
                for s in range(2):
                    maxima(L * ST, s, 0)
                    shifts(L * ST, L * AT, s, 0)
                v_copy(L * AT, 0, 0)
                inverses(L * ST, 0)
                normalise(L * ST, 0, 0)
                with dve.Fori(0, B) as j:
                    for par in range(2):
                        t = j * 2 + par
                        tile(L * ST + t * PAIRS, L * AT + t + 1, L * (NT + 1) + t, par, bass.ds(t, 1), L * B + j)
                v_copy(L * AT + NT, 1, 0)
                inverses(L * ST + NT * PAIRS, 1)
                normalise(L * ST + NT * PAIRS, 1, 0)
                update(L * (NT + 1) + NT, bass.ds(NT, 1))
                dve.wait_ge(ffn_w_in, (L + 1) * (16 * N_FFN))
                nc.vector.tensor_scalar(w1g[:], w1[:], lng[:, 0:1], None, ALU.mult)
                nc.vector.tensor_copy(lnb_l[:], lnb[:, 0:1].to_broadcast([P, P])).then_inc(w1g_done, 1)
                dve.wait_ge(x_upd, (L + 1) * (NT + 1) + CR)
                dve.wait_ge(bias_mm, L + (1 + CR))
                nc.vector.tensor_tensor(bias1[:, 0:F], bank[5][:, 0:F], b1r[:, 0:F], ALU.add)
                nc.vector.tensor_tensor(bias1[:, F:2 * F], bank[6][:, 0:F], b1r[:, F:2 * F], ALU.add).then_inc(bias_done, 1)

                def front(k, slot, at):
                    nc.vector.tensor_copy(xsf[:], x[:, at, :]).then_inc(f_xs, 1)
                    nc.vector.tensor_tensor(xbf[:, slot], x[:, at, :], b2r[:, None, :].to_broadcast([P, FT, D]),
                                            ALU.add).then_inc(f_xb, 1)

                def biased(n, k, slot, i):
                    if i == 0:
                        dve.wait_ge(f_rstd, k + (1 + CR))
                    dve.wait_ge(f_h, L * (NT + 2) + n + (1 + CR))
                    dve.wait_ge(f_hm, L * NT + n + (CR - 1))
                    ba, bg = FH[i % 2]
                    nc.vector.scalar_tensor_tensor(out=hg[:, i % 2, :], in0=bg[:, 0:F], scalar=rsf[:, slot, i:i + 1],
                                                   in1=bias1[:, F:2 * F], op0=ALU.mult, op1=ALU.add)
                    nc.vector.scalar_tensor_tensor(out=ha[:, i % 2, :], in0=ba[:, 0:F], scalar=rsf[:, slot, i:i + 1],
                                                   in1=bias1[:, 0:F], op0=ALU.mult, op1=ALU.add).then_inc(f_hb, 1)

                front(L * (NF + 1), 0, bass.ds(1, FT))
                biased(0, L * (NF + 1), 0, 0)
                with dve.Fori(0, NF // 2) as f:
                    for slot in range(2):
                        k = L * (NF + 1) + f * 2 + slot
                        r = L * NF + f * 2 + slot
                        dve.wait_ge(f_xT, k + (1 + CR))
                        dve.wait_ge(x_full, (L + 1) * B + (f * 2 + slot) * 2)
                        front(k + 1, 1 - slot, bass.ds((f * 2 + slot + 1) * FT + 1, FT))
                        for i in range(1, FT + 1):
                            n = (f * 2 + slot) * FT + i
                            if i < FT:
                                biased(n, k, slot, i)
                            else:
                                biased(n, k + 1, 1 - slot, 0)
                        dve.wait_ge(f_z, r + (1 + CR))
                        dve.wait_ge(f_xb, k + (1 + CR))
                        nc.vector.tensor_tensor(x[:, bass.ds((f * 2 + slot) * FT + 1, FT), :], FZ[:].rearrange("p (t d) -> p t d", t=FT),
                                                xbf[:, slot], ALU.add).then_inc(x_full, 2)
            dve.wait_ge(x_full, (DEPTH + 1) * B)
            for i in range(4):
                xv = x[:, 1 + i * NT // 4:1 + (i + 1) * NT // 4, :].rearrange("p (b t) d -> p b t d", t=TPB)
                nc.vector.tensor_tensor(xv, xv, gb[:, i * B // 4:(i + 1) * B // 4, None, :].to_broadcast([P, B // 4, TPB, D]),
                                        ALU.mult).then_inc(scaled, 1)
            for i in range(4):
                part = slice(i * NT // 4, (i + 1) * NT // 4)
                xo = x[:, 1 + i * NT // 4:1 + (i + 1) * NT // 4, :]
                dve.wait_ge(scaled, i + 1)
                nc.vector.tensor_tensor(xo, xo, x1[:, part, :], ALU.add).then_inc(gated, 1)

        @block.tensor
        def _(pe):
            for s in (xT_done, chunk_done, rot_turned, sims_done, pt_done, pv_done, wo_done,
                      w1c_mm, bias_mm, f_xT, f_yc, f_h, f_hT, f_z):
                pe.sem_inc(s, CR)
            mm = nc.tensor.matmul
            pe.wait_ge(const_in, 16 * N_CONST)
            pe.wait_ge(dve_setup, 10)
            pe.wait_ge(pool_setup, POOL_SETUP)
            nc.tensor.transpose(bank[0][:, 0:B], crow[:], ident[0:B, 0:B]).then_inc(pe_setup, 1)

            with pe.Fori(0, B // 2) as j:
                for u in range(2):
                    pe.wait_ge(m_dve[u], j * DA + 1)
                    mm(bank[0 + 4 * u][:, 0:3 * D], cb_l[u][:], wmod_s[:, 0:3 * D], start=True, stop=True)
                    mm(bank[1 + 4 * u][:, 0:3 * D], cb_l[u][:], wmod_s[:, 3 * D:6 * D], start=True, stop=True).then_inc(m_pe[u], 1)
                for u in range(2):
                    pe.wait_ge(m_dve[u], j * DA + 12)
                    for t in range(TPB):
                        last = nc.tensor.transpose(bank[2 + 4 * u][:, t * P:(t + 1) * P], h1s[u][:, t, :], ident[:])
                    last.then_inc(m_pe[u], 1)
                for u in range(2):
                    pe.wait_ge(m_act[u], j * AA + 4)
                    mm(bank[3 + 4 * u][:, 0:S], w1q[:], h1T[u][:], start=True, stop=True)
                    mm(bank[0 + 4 * u][:, 0:S], w1k[:], h1T[u][:], start=True, stop=True)
                    for t in range(TPB):
                        last = mm(bank[1 + 4 * u][:, t * D:(t + 1) * D], h1T[u][:, t * P:(t + 1) * P], w1v[:], start=True, stop=True)
                    last.then_inc(m_pe[u], 1)
                for u in range(2):
                    pe.wait_ge(m_act[u], j * AA + 6)
                    for q, k, at in ((0, 0, 0), (1, 0, 1), (1, 1, 2)):
                        o = bank[2 + 4 * u][:, at * P:(at + 1) * P]
                        if q == k:
                            mm(o, identb[:], mask_causal, start=True, stop=False)
                        last = mm(o, q1T[u][:, q * P:(q + 1) * P], k1T[u][:, k * P:(k + 1) * P], start=(q != k), stop=True)
                    last.then_inc(m_pe[u], 1)
                for u in range(2):
                    pe.wait_ge(m_dve[u], j * DA + 19)
                    for i in range(3):
                        last = nc.tensor.transpose(bank[3 + 4 * u][:, i * P:(i + 1) * P], p1[u][:, i * P:(i + 1) * P], ident[:])
                    last.then_inc(m_pe[u], 1)
                for u in range(2):
                    pe.wait_ge(m_act[u], j * AA + 9)
                    mm(bank[0 + 4 * u][:, 0:P], v1[u][:, 0, :], p1T[u][:, 0:P], start=True, stop=True)
                    mm(bank[0 + 4 * u][:, P:S], v1[u][:, 0, :], p1T[u][:, P:2 * P], start=True, stop=False)
                    mm(bank[0 + 4 * u][:, P:S], v1[u][:, 1, :], p1T[u][:, 2 * P:3 * P], start=False, stop=True).then_inc(m_pe[u], 1)
                for u in range(2):
                    pe.wait_ge(m_act[u], j * AA + 10)
                    for t in range(TPB):
                        last = mm(bank[1 + 4 * u][:, t * D:(t + 1) * D], o1T[u][:, t * P:(t + 1) * P], w1o[:], start=True, stop=True)
                    last.then_inc(m_pe[u], 1)

            def x_turn(y):
                pe.wait_ge(xs_ready, y + (1 + CR))
                nc.tensor.transpose(T[:, 0:P], xs[:], ident[:]).then_inc(xT_done, 1)

            def chunk(a, y, c, par):
                if c == 0:
                    pe.wait_ge(yT_ready, y + (1 + CR))
                if c < 2:
                    pe.wait_ge(v_done, a * 2 + (c - 1 + CR))
                else:
                    pe.wait_ge(prod_done, a * KQ + (c - 1 + CR))
                mm(G[c % 2][:], yT[:, par, 0:P], wqkv[:, CHUNK_COL[c]:CHUNK_COL[c] + CH],
                   start=True, stop=True).then_inc(chunk_done, 1)

            def turn(a, c):
                if c % 2 == 0:
                    pe.wait_ge(rsum_done, a * KQ + (c + 1 + CR))
                    src = rsq[:, c // 2, :]
                else:
                    pe.wait_ge(rot_done, a * 2 + (c // 2 + 1 + CR))
                    src = rot[:, c // 2, :]
                for i in range(4):
                    last = nc.tensor.transpose(T[:, i * P:(i + 1) * P], src[:, i * P:(i + 1) * P], ident[:])
                last.then_inc(rot_turned, 1)

            def sims(e, a, s, par, batch):
                if s == 0:
                    pe.wait_ge(t_copied, a * KQ + (2 + CR))
                    if par:
                        pe.wait_ge(ktail_done, batch + (1 + CR))
                if s == 4:
                    pe.wait_ge(t_copied, a * KQ + (4 + CR))
                pe.wait_ge(exp_done, e + (s - 1 + CR))
                N = WIDE if par else P
                kT, mask = (kTo, mask_odd) if par else (kTe, mask_even)
                bk = SIM[s % 2]
                mm(bk[:, 0:2 * N].rearrange("p (h n) -> p h n", h=2), identb[:], mask[:, None, :].to_broadcast([P, 2, N]),
                   start=True, stop=False, skip_group_check=True)
                for h in range(2):
                    last = mm(bk[:, h * N:(h + 1) * N], qT[:, par, h, s, :], kT[:, s, :], start=False, stop=(h == 1),
                              skip_group_check=True)
                last.then_inc(sims_done, 1)

            def p_turn(e, g, s, par):
                pe.wait_ge(norm_done, e + (s + 1 + CR))
                pe.wait_ge(pt_copied, g + (s + CR))
                slot = s % 2
                own = WIN if par else 0
                for h in range(2):
                    last = nc.tensor.transpose(PT[:, h * P:(h + 1) * P], pr[:, slot, h, own:own + P], ident[:])
                if par:
                    for h in range(2):
                        last = nc.tensor.transpose(PT[0:WIN, 2 * P + h * WIN:2 * P + (h + 1) * WIN], pr[0:WIN, slot, h, 0:WIN],
                                                   ident[0:WIN, 0:WIN])
                last.then_inc(pt_done, 1)

            def outputs(g, a, u, s, par, batch):
                pe.wait_ge(pt_copied, g + (s + 1 + CR))
                if s == 0:
                    pe.wait_ge(v_done, a * 2 + (1 + CR))
                    if par:
                        pe.wait_ge(vtail_done, batch * 16 + 16)
                if s == 4:
                    pe.wait_ge(v_done, a * 2 + (2 + CR))
                if s % 4 == 0:
                    pe.wait_ge(o_copied, u + (s // 4 + 1 + CR))
                slot, col = s % 2, (s % 4) * P
                for h in range(2):
                    head = slice((2 * s + h) * DH, (2 * s + h + 1) * DH)
                    half = slice(h * DH, (h + 1) * DH)
                    last = mm(O[half, col:col + P], v[:, par, head], pT[:, slot, h * P:(h + 1) * P], start=True, stop=not par,
                              skip_group_check=True)
                    if par:
                        last = mm(O[half, col:col + WIN], vt[:, head], pT[0:WIN, slot, 2 * P + h * WIN:2 * P + (h + 1) * WIN],
                                  start=False, stop=True, skip_group_check=True)
                last.then_inc(pv_done, 1)

            def project(u, w):
                pe.wait_ge(o_copied, u + (1 + CR))
                pe.wait_ge(x_upd, w + CR)
                for c in range(PAIRS):
                    last = mm(Z[:, 0:D], oT[:, c, :], wo[:, c, :], start=(c == 0), stop=(c == PAIRS - 1))
                last.then_inc(wo_done, 1)

            def tile(e, b, a, y, w, u, par, batch):
                g = b * PAIRS
                nxt = 1 - par
                chunk_of = {0: 0, 1: 1, 3: 2, 4: 3, 6: 4, 7: 5}
                for s in range(PAIRS):
                    if s + 2 < PAIRS:
                        sims(e, a - 1, s + 2, par, batch)
                    if s in chunk_of:
                        chunk(a, y, chunk_of[s], nxt)
                    if s == 6:
                        outputs(g, a - 1, u, 4, par, batch)
                    p_turn(e, g, s, par)
                    if s + 2 >= PAIRS:
                        sims(e + PAIRS, a, s + 2 - PAIRS, nxt, batch)
                    if s == 0:
                        pe.wait_ge(t_copied, a * KQ + (CR - 1))
                        turn(a - 1, 3)
                    if s == 3:
                        pe.wait_ge(t_copied, a * KQ + CR)
                        x_turn(y + 1)
                    if s == 4:
                        pe.wait_ge(yT_ready, y + (2 + CR))
                        turn(a, 0)
                    if s == 5:
                        pe.wait_ge(t_copied, a * KQ + (1 + CR))
                        turn(a, 1)
                    if s == 7:
                        pe.wait_ge(t_copied, a * KQ + (2 + CR))
                        turn(a, 2)
                    if s >= 1 and s != 5:
                        outputs(g, a - 1, u, s - 1, par, batch)
                    if s == 2:
                        project(u, w)
                outputs(g, a - 1, u, PAIRS - 1, par, batch)

            with pe.Fori(0, DEPTH) as L:
                pe.wait_ge(x_full, (L + 1) * B)
                pe.wait_ge(attn_w_in, (L + 1) * (16 * N_ATTN))
                x_turn(L * YT)
                for c in range(6):
                    chunk(L * AT, L * YT, c, 0)
                turn(L * AT, 0)
                pe.wait_ge(t_copied, L * (AT * KQ) + (1 + CR))
                turn(L * AT, 1)
                pe.wait_ge(t_copied, L * (AT * KQ) + (2 + CR))
                x_turn(L * YT + 1)
                pe.wait_ge(yT_ready, L * YT + (2 + CR))
                turn(L * AT, 2)
                sims(L * ST, L * AT, 0, 0, L * B)
                sims(L * ST, L * AT, 1, 0, L * B)
                with pe.Fori(0, B) as j:
                    for par in range(2):
                        t = j * 2 + par
                        tile(L * ST + t * PAIRS, L * NT + t, L * AT + t + 1, L * YT + t + 1, L * (NT + 1) + t, L * OT + t * 2, par,
                             L * B + j)
                pe.wait_ge(t_copied, (L + 1) * (AT * KQ) + (CR - 1))
                turn(L * AT + NT, 3)
                project((L + 1) * OT - 1, L * (NT + 1) + NT)
                pe.wait_ge(x_upd, (L + 1) * (NT + 1) + CR)
                pe.wait_ge(exp_done, (L + 1) * ST + CR)
                pe.wait_ge(v_done, (L + 1) * (2 * AT) + CR)
                pe.wait_ge(t_copied, (L + 1) * (KQ * AT) + CR)
                pe.wait_ge(w1g_done, L + (1 + CR))
                for i in range(2):
                    last = mm(bank[i][:, 0:F], center[:], w1g[:, i * F:(i + 1) * F], start=True, stop=True)
                last.then_inc(w1c_mm, 1)
                for i in range(2):
                    last = mm(bank[5 + i][:, 0:F], lnb_l[:], w1[:, i * F:(i + 1) * F], start=True, stop=True)
                last.then_inc(bias_mm, 1)
                pe.wait_ge(w1c_done, L + (1 + CR))
                pe.wait_ge(bias_done, L + (1 + CR))

                def x_turns(k):
                    pe.wait_ge(f_xs, k + (1 + CR))
                    for i in range(FT):
                        last = nc.tensor.transpose(FT_B[:, i * P:(i + 1) * P], xsf[:, i, :], ident[:])
                    last.then_inc(f_xT, 1)

                def centred_rows(k, slot):
                    pe.wait_ge(f_yT, k + (1 + CR))
                    pe.wait_ge(f_ss, k * FT + CR)
                    for i in range(FT):
                        last = mm(FYC[:, i * P:(i + 1) * P], yTf[:, slot, i // TPB, (i % TPB) * P:(i % TPB + 1) * P], center[:],
                                  start=True, stop=True)
                    last.then_inc(f_yc, 1)

                def hidden(n, slot, i):
                    pe.wait_ge(f_hb, L * (NT + 1) + n + (CR - 1))
                    for half in (1, 0):
                        last = mm(FH[i % 2][half][:, 0:F], yTf[:, slot, i // TPB, (i % TPB) * P:(i % TPB + 1) * P],
                                  w1c[:, half * F:(half + 1) * F], start=True, stop=True)
                    last.then_inc(f_h, 1)

                def hidden_turn(m, i):
                    pe.wait_ge(f_hm, m + (i + 1 + CR))
                    pe.wait_ge(f_hTc, m + (i + CR))
                    for c, (at, size) in enumerate(FCH):
                        last = nc.tensor.transpose(FHT[0:size, c * P:(c + 1) * P], hm[:, i % 2, at:at + size], ident[:])
                    last.then_inc(f_hT, 1)

                def down(m, i):
                    pe.wait_ge(f_hTc, m + (i + 1 + CR))
                    for c, (at, size) in enumerate(FCH):
                        last = mm(FZ[:, i * D:(i + 1) * D], hT[0:size, i % 2, c * P:(c + 1) * P], w2[0:size, c, :],
                                  start=(c == 0), stop=(c == 2))
                    return last

                x_turns(L * (NF + 1))
                centred_rows(L * (NF + 1), 0)
                pe.wait_ge(f_hb, L * (NT + 1) + CR)
                hidden(0, 0, 0)
                hidden(1, 0, 1)
                with pe.Fori(0, NF // 2) as f:
                    for slot in range(2):
                        k = L * (NF + 1) + f * 2 + slot
                        m = (L * NF + f * 2 + slot) * FT
                        n = (f * 2 + slot) * FT
                        hidden_turn(m, 0)
                        x_turns(k + 1)
                        hidden(n + 2, slot, 2)
                        centred_rows(k + 1, 1 - slot)
                        hidden_turn(m, 1)
                        hidden(n + 3, slot, 3)
                        pe.wait_ge(x_full, (L + 1) * B + (f * 2 + slot) * 2)
                        down(m, 0)
                        hidden_turn(m, 2)
                        hidden(n + 4, 1 - slot, 0)
                        down(m, 1)
                        hidden_turn(m, 3)
                        down(m, 2)
                        hidden(n + 5, 1 - slot, 1)
                        down(m, 3).then_inc(f_z, 1)


def _constants():
    f32 = np.float32
    ident = np.eye(P, dtype=f32)
    q = np.arange(P)[:, None]
    even = np.arange(P)[None, :]
    odd = np.arange(WIDE)[None, :] - WIN
    band = lambda k: np.where((k > q) | (k < q - WIN), f32(MASKED), f32(0))
    masks = np.concatenate([band(even), band(odd), np.where(even > q, f32(MASKED), f32(0))], 1).astype(f32)
    center = (ident - f32(1.0 / D)).astype(f32)
    half = np.arange(0, DH, 2, dtype=f32)
    inv_freq = f32(1.0) / np.power(f32(10000.0), half / f32(DH), dtype=f32)
    t = np.arange(S, dtype=f32)
    freqs = t[:, None] * inv_freq[None, :]
    freqs = np.concatenate([freqs, freqs], -1)
    base = (half + f32(0.4 * DH)) / f32(1.4 * DH)
    power = (t - f32(S // 2)) / f32(WIN // 2)
    scale = np.power(base[None, :], power[:, None], dtype=f32)
    scale = np.concatenate([scale, scale], -1)
    sign = np.where(np.arange(DH) < DH // 2, f32(-1), f32(1))
    cos, sin = np.cos(freqs).astype(f32), np.sin(freqs).astype(f32) * sign
    inv = f32(1.0) / scale
    rope = np.stack([cos * inv, sin * inv, cos * scale * f32(QK_SCALE), sin * scale * f32(QK_SCALE)], 0)
    rope = rope.reshape(4, TPB, P, DH).transpose(2, 0, 1, 3)
    return {"ident": ident, "masks": masks, "center": center, "rope": np.ascontiguousarray(rope.astype(f32))}


_INS = ['L0_attn_x', 'L0_attn_Wq', 'L0_attn_Wk', 'L0_attn_Wv', 'L0_attn_Wo', 'L0_ffn_Wqkv', 'L0_ffn_q_scale',
        'L0_ffn_k_scale', 'L0_ffn_Wo', 'L0_ffn_ln_g', 'L0_ffn_ln_b', 'L0_ffn_W1', 'L0_ffn_b1', 'L0_ffn_W2',
        'L0_ffn_b2', 'L0_c', 'L0_wmod']


def kernel(**inputs):
    import concourse.bacc as bacc
    from concourse.bass_utils import run_bass_kernel_spmd as run

    nc = bacc.Bacc("TRN2", target_bir_lowering=False, num_devices=1)
    arrays, args = {}, []
    named = [(n, np.ascontiguousarray(inputs[n])) for n in _INS] + list(_constants().items())
    for name, a in named:
        arrays[f"in_{name}"] = a
        args.append(nc.dram_tensor(f"in_{name}", a.shape, mybir.dt.from_np(a.dtype), kind="ExternalInput").ap())
    args.append(nc.dram_tensor("out_0", (B, S, D), F32, kind="ExternalOutput").ap())
    build(nc, *args)
    r = run(nc, [arrays], core_ids=[0])
    return r.results[0]["out_0"]
```
